# Optimizing a Trainium2 kernel written in Bass

```python
import numpy as np
import jax
import jax.numpy as jnp

def _softmax(x, axis=-1):
    return jax.nn.softmax(x, axis=axis)

def _gelu(x):
    return jax.nn.gelu(x, approximate=True)

def _silu(x):
    return jax.nn.silu(x)

def _sigmoid(x):
    return jax.nn.sigmoid(x)

def _layernorm(x, axis=-1, eps=1e-05):
    m = jnp.mean(x, axis=axis, keepdims=True)
    v = jnp.var(x, axis=axis, keepdims=True)
    return (x - m) / jnp.sqrt(v + eps)

def _scatter_add(tgt, idx, src, axis=0):
    return tgt.at[idx].add(src)

def _segment_sum(src, seg, n):
    return jax.ops.segment_sum(src, seg, n)
kernel_name = 'mk_seq_preln_d1_jaxref_r8_8da034'

def setup_inputs(seed: int=0):
    np.random.seed(seed)
    _w = jnp.asarray

    def _L0_attn_setup():
        import jax, jax.numpy as jnp
        import numpy as np
        import math
        NUM_HEADS = 8
        EMB = 128
        HEAD_DIM = 128
        B, T = (1, 512)

        def sinusoidal_pe(T, d, dtype=jnp.float32):
            pos = jnp.arange(T, dtype=dtype)[:, None]
            inv_freq = jnp.exp(-math.log(10000.0) * jnp.arange(0, d, 2, dtype=dtype) / d)
            ang = pos * inv_freq[None, :]
            pe = jnp.zeros((T, d), dtype=dtype)
            pe = pe.at[:, 0::2].set(jnp.sin(ang))
            pe = pe.at[:, 1::2].set(jnp.cos(ang))
            return pe
        key = jax.random.key(seed)
        ks = jax.random.split(key, 6)
        s = lambda fan_in: 1.0 / math.sqrt(fan_in)
        x = jax.random.normal(ks[0], (B, T, EMB), dtype=jnp.float32)
        Wq = jax.random.normal(ks[1], (EMB, NUM_HEADS * HEAD_DIM), dtype=jnp.float32) * s(EMB)
        bq = jax.random.normal(ks[2], (NUM_HEADS * HEAD_DIM,), dtype=jnp.float32) * s(EMB)
        Wkv = jax.random.normal(ks[3], (EMB, 2 * HEAD_DIM), dtype=jnp.float32) * s(EMB)
        bkv = jax.random.normal(ks[4], (2 * HEAD_DIM,), dtype=jnp.float32) * s(EMB)
        Wo = jax.random.normal(ks[5], (NUM_HEADS * HEAD_DIM, EMB), dtype=jnp.float32) * s(NUM_HEADS * HEAD_DIM)
        return {'x': x, 'Wq': Wq, 'bq': bq, 'Wkv': Wkv, 'bkv': bkv, 'Wo': Wo}
    _L0_attn_in = _L0_attn_setup()

    def _L0_ffn_setup():
        import jax, jax.numpy as jnp
        import numpy as np
        NUM_EXPERTS_TOTAL = 9
        TOP_K = 2
        key = jax.random.key(seed)
        k0, k1, k2, k3, k4 = jax.random.split(key, 5)
        B, S, H, I = (2, 256, 128, 352)
        E = NUM_EXPERTS_TOTAL
        x = jax.random.normal(k0, (B, S, H), dtype=jnp.float32)
        Wr = jax.random.normal(k1, (H, E), dtype=jnp.float32) * 0.02
        Wg = jax.random.normal(k2, (E, H, I), dtype=jnp.float32) * 0.02
        Wu = jax.random.normal(k3, (E, H, I), dtype=jnp.float32) * 0.02
        Wd = jax.random.normal(k4, (E, I, H), dtype=jnp.float32) * 0.02
        return {'x': x, 'Wr': Wr, 'Wg': Wg, 'Wu': Wu, 'Wd': Wd}
    _L0_ffn_in = _L0_ffn_setup()
    _d = {'L0_attn_x': _L0_attn_in['x'], 'L0_attn_Wq': _L0_attn_in['Wq'], 'L0_attn_bq': _L0_attn_in['bq'], 'L0_attn_Wkv': _L0_attn_in['Wkv'], 'L0_attn_bkv': _L0_attn_in['bkv'], 'L0_attn_Wo': _L0_attn_in['Wo'], 'L0_ffn_Wr': _L0_ffn_in['Wr'], 'L0_ffn_Wg': _L0_ffn_in['Wg'], 'L0_ffn_Wu': _L0_ffn_in['Wu'], 'L0_ffn_Wd': _L0_ffn_in['Wd']}
    _x0 = _d['L0_attn_x']
    _d['L0_attn_x'] = jax.random.normal(jax.random.fold_in(jax.random.key(seed), 1), (8, 512, 128), dtype=_x0.dtype)
    del _x0
    return _d

def reference(L0_attn_x, L0_attn_Wq, L0_attn_bq, L0_attn_Wkv, L0_attn_bkv, L0_attn_Wo, L0_ffn_Wr, L0_ffn_Wg, L0_ffn_Wu, L0_ffn_Wd):

    def _L0_attn_ref(x, Wq, bq, Wkv, bkv, Wo):
        import jax, jax.numpy as jnp
        import numpy as np
        import math
        NUM_HEADS = 8
        EMB = 128
        HEAD_DIM = 128
        B, T = (1, 512)

        def sinusoidal_pe(T, d, dtype=jnp.float32):
            pos = jnp.arange(T, dtype=dtype)[:, None]
            inv_freq = jnp.exp(-math.log(10000.0) * jnp.arange(0, d, 2, dtype=dtype) / d)
            ang = pos * inv_freq[None, :]
            pe = jnp.zeros((T, d), dtype=dtype)
            pe = pe.at[:, 0::2].set(jnp.sin(ang))
            pe = pe.at[:, 1::2].set(jnp.cos(ang))
            return pe
        Bsz, Tlen, E = x.shape
        q = (x @ Wq + bq).reshape(Bsz, Tlen, NUM_HEADS, HEAD_DIM)
        kv = x @ Wkv + bkv
        k, v = (kv[..., :HEAD_DIM], kv[..., HEAD_DIM:])
        q = jnp.transpose(q, (0, 2, 1, 3))
        pe = sinusoidal_pe(Tlen, HEAD_DIM, x.dtype)
        q = q + pe[None, None, :, :]
        k = k + pe[None, :, :]
        scale = 1.0 / math.sqrt(HEAD_DIM)
        scores = jnp.einsum('bhqd,bkd->bhqk', q, k) * scale
        causal = jnp.tril(jnp.ones((Tlen, Tlen), dtype=bool))
        scores = jnp.where(causal[None, None, :, :], scores, jnp.finfo(scores.dtype).min)
        probs = jax.nn.softmax(scores, axis=-1)
        attn = jnp.einsum('bhqk,bkd->bhqd', probs, v)
        out = jnp.transpose(attn, (0, 2, 1, 3)).reshape(Bsz, Tlen, NUM_HEADS * HEAD_DIM)
        return out @ Wo

    def _L0_ffn_ref(x, Wr, Wg, Wu, Wd):
        import jax, jax.numpy as jnp
        import numpy as np
        NUM_EXPERTS_TOTAL = 9
        TOP_K = 2
        B, S, H = x.shape
        E = NUM_EXPERTS_TOTAL
        T = B * S
        logits = jnp.einsum('bsh,he->bse', x, Wr)
        probs = jax.nn.softmax(logits, axis=-1)
        topk_w, topk_idx = jax.lax.top_k(probs, TOP_K)
        topk_w = topk_w / jnp.sum(topk_w, axis=-1, keepdims=True)
        xf = x.reshape(T, H)
        wf = topk_w.reshape(T, TOP_K)
        idxf = topk_idx.reshape(T, TOP_K)
        cw = jnp.zeros((T, E), dtype=x.dtype).at[jnp.arange(T)[:, None], idxf].add(wf)
        gate = jax.nn.silu(jnp.einsum('th,ehi->tei', xf, Wg))
        hidden = gate * jnp.einsum('th,ehi->tei', xf, Wu)
        out = jnp.einsum('tei,eih,te->th', hidden, Wd, cw)
        return out.reshape(B, S, H)
    x = L0_attn_x
    x = x + _L0_attn_ref(_layernorm(x, axis=-1), L0_attn_Wq, L0_attn_bq, L0_attn_Wkv, L0_attn_bkv, L0_attn_Wo)
    x = x + _L0_ffn_ref(_layernorm(x, axis=-1), L0_ffn_Wr, L0_ffn_Wg, L0_ffn_Wu, L0_ffn_Wd)
    return x

_drawn_inputs = setup_inputs


def setup_inputs(seed=0):
    import zlib

    import numpy as np

    out = dict(_drawn_inputs(seed))
    spreads = {}
    factors = {'L0_attn_bq': 2.984,
     'L0_ffn_Wr': 8.0,
     'L0_ffn_Wg': 8.0,
     'L0_ffn_Wu': 8.0,
     'L0_ffn_Wd': 8.0}
    for name, (base, spread) in spreads.items():
        noise = np.random.default_rng([zlib.crc32(name.encode()), seed]).standard_normal(out[name].shape)
        drawn = base * np.exp(spread * noise) if base else spread * noise
        out[name] = jnp.asarray(drawn.astype(out[name].dtype))
    for name, factor in factors.items():
        out[name] = (out[name] * factor).astype(out[name].dtype)
    return out
```

```python
from contextlib import ExitStack

import numpy as np

import concourse.bass as bass
from concourse import mybir

F32, BF16, I32 = mybir.dt.float32, mybir.dt.bfloat16, mybir.dt.int32
ALU = mybir.AluOpType
ACT = mybir.ActivationFunctionType
AX = mybir.AxisListType

B, T, D = 8, 512, 128
H = 8
QT = T // 128
NTOK = B * T
NT = NTOK // 128
E, I, TOPK = 9, 352, 2
IC = 3
IP = IC * 128
SCALE = float(D) ** -0.5
EPS = 1e-5
NEG = -1.0e30
BIG = 3.0e38

ROW = D + 2
CAP = NTOK + 128
TILES = TOPK * NTOK // 128 + E - 1 + (-(TOPK * NTOK // 128 + E - 1)) % 6
SPARE = TILES - TOPK * NTOK // 128
PADS = E + SPARE
XS_ROWS = E * CAP + SPARE * 128
Y_ROWS = TOPK * NTOK + PADS * 128
SCATTERS = QT * TOPK
NX = 6
GROUPS = TILES // NX
STEPS = H * QT + 2 * 2 + 1 + (1 + 5 * TOPK + 1) + (3 + 1 + 2 * TOPK + 1)

C_ID = 0
C_MASK = C_ID + 128
C_LT = C_MASK + T
C_ONE = C_LT + 128
C_REV = C_ONE + 128
C_THR = C_REV + QT * E
C_LE = C_THR + NT
C_J = C_LE + E * E
C_CAP = C_J + TILES
C_POW = C_CAP + E
C_END = C_POW + QT


def constants():
    c = np.zeros((128, C_END), np.float32)
    p = np.arange(128)
    c[:, C_ID:C_ID + 128] = np.eye(128)
    c[:, C_MASK + T - 128:C_MASK + T] = np.where(p[None, :] > p[:, None], NEG, 0.0)
    c[:, C_LT:C_LT + 128] = p[:, None] < p[None, :]
    c[:, C_ONE:C_ONE + 128] = 1.0
    c[:, C_REV:C_REV + QT * E] = np.tile(E - np.arange(E), QT)
    c[:, C_THR:C_THR + NT] = 128 * np.arange(NT)
    c[:, C_LE:C_LE + E * E] = (np.arange(E)[None, :] <= np.arange(E)[:, None]).reshape(-1)
    c[:, C_J:C_J + TILES] = np.arange(TILES)
    c[:, C_CAP:C_CAP + E] = CAP * np.arange(E)
    c[:, C_POW:C_POW + QT] = -0.5
    t, k = np.arange(QT)[:, None], np.arange(TOPK)[None, :]
    pairs = (k * NTOK + t * 128 - T).reshape(1, -1) + p[:, None]
    pads = TOPK * NTOK + 128 * np.arange(PADS)[None, :] + p[:, None]
    dest = np.concatenate([pairs, pads], 1).astype(np.int32)
    pos = np.arange(T, dtype=np.float32)[:, None]
    inv = np.exp(np.float32(-np.log(10000.0)) * np.arange(0, D, 2, dtype=np.float32) / np.float32(D))
    ang = pos * inv[None, :].astype(np.float32)
    pe = np.zeros((T, D), np.float32)
    pe[:, 0::2] = np.sin(ang)
    pe[:, 1::2] = np.cos(ang)
    return c, dest, np.ascontiguousarray(pe.T)


def block_kernel(nc, x, wq, bq, wkv, bkv, wo, wr, wg, wu, wd, consts, dest, positions, out):
    ctx = ExitStack()
    with ctx:
        def sb(name, shape, dt=F32):
            return ctx.enter_context(nc.sbuf_tensor(name, shape, dt))

        def sem(name):
            return ctx.enter_context(nc.semaphore(name))

        xs_dram = nc.dram_tensor("xs_dram", (XS_ROWS, ROW), F32, kind="Internal").ap()
        y_dram = nc.dram_tensor("y_dram", (Y_ROWS, D), F32, kind="Internal").ap()

        cst = sb("cst", [128, C_END])
        dst0 = sb("dst0", [128, SCATTERS + PADS], I32)
        pe_sb = sb("pe_sb", [128, T])
        wq_sb = sb("wq_sb", [128, H * D])
        wkv_sb = sb("wkv_sb", [128, 2 * D])
        wo_sb = sb("wo_sb", [128, H * D])
        wr_sb = sb("wr_sb", [128, E])
        bq_sb = sb("bq_sb", [128, H])
        bkv_sb = sb("bkv_sb", [128, 2])
        wgu_sb = sb("wgu_sb", [128, E, 2 * I])
        wd_sb = sb("wd_sb", [128, E, IC, D])
        lt_bf = sb("lt_bf", [128, 128], BF16)
        one_bf = sb("one_bf", [128, 128], BF16)
        ident = cst[:, C_ID:C_ID + 128]

        x_all = sb("x_all", [128, NT * D])
        stats = sb("stats", [128, QT, 6])
        mv = sb("mv", [128, QT, 2])
        veps = sb("veps", [128, 2, QT])
        rstd = sb("rstd", [128, 2, QT])
        xn = sb("xn", [128, QT, D])
        xnT = sb("xnT", [128, T])
        kT = sb("kT", [128, T])
        vT = sb("vT", [128, T])
        vw = sb("vw", [128, QT, H * D])
        qT = sb("qT", [128, 2, T])
        negs = sb("negs", [128, QT, T])
        nmax = sb("nmax", [128, 2, QT])
        rsum = sb("rsum", [128, 2, QT])
        rinv = sb("rinv", [128, 2, QT])
        pr = sb("pr", [128, 2, QT, T])
        pT = sb("pT", [128, 2, QT, T])
        oT = sb("oT", [128, T])

        payload = sb("payload", [128, QT, TOPK, ROW])
        stats2 = sb("stats2", [128, QT, 6])
        mv2 = sb("mv2", [128, QT, 2])
        xn2T = sb("xn2T", [128, T])
        lg = sb("lg", [128, TOPK, QT * E])
        top = sb("top", [128, TOPK, QT])
        iseq = sb("iseq", [128, QT * E])
        key = sb("key", [128, QT * E])
        kmax = sb("kmax", [128, QT])
        oh = sb("oh", [128, TOPK, QT * E])
        oh_bf = sb("oh_bf", [128, QT * E], BF16)
        gap = sb("gap", [128, QT])
        e2 = sb("e2", [128, QT])
        den = sb("den", [128, QT])
        wrow = sb("wrow", [128, QT, TOPK])
        pos = sb("pos", [128, QT * E])
        posk = sb("posk", [128, TOPK, QT * E])
        slot_f = sb("slot_f", [128, TOPK, QT])
        slot = sb("slot", [128, TOPK, QT], I32)
        fill = sb("fill", [128, E])
        padrows = sb("padrows", [128, PADS, ROW])
        cnt = sb("cnt", [128, E])
        over = sb("over", [128, E * NT])
        ntile = sb("ntile", [128, E])
        cumm = sb("cumm", [128, E * E])
        cum = sb("cum", [128, E])
        done = sb("done", [128, TILES * E])
        skip = sb("skip", [128, TILES * E])
        ej = sb("ej", [128, TILES])
        st = sb("st", [128, TILES])
        rowf = sb("rowf", [128, TILES])
        row_tab = sb("row_tab", [128, TILES], I32)
        e_tab = sb("e_tab", [128, TILES], I32)
        fill_i = sb("fill_i", [128, E], I32)

        xs = sb("xs", [128, NX, ROW])
        xsT = sb("xsT", [128, 2, D])
        sg = sb("sg", [128, 2, I])
        hid = sb("hid", [128, 2, IP])
        hidT = sb("hidT", [128, 2, IP])
        ys = sb("ys", [128, NX, D])
        y_in = [[pr[:, 0, c, :], pr[:, 1, c, :]] for c in range(QT)] + \
               [[pT[:, 0, c, :], pT[:, 1, c, :]] for c in range(QT)]

        bank = [ctx.enter_context(nc.psum_tensor(f"bank{i}", [128, 512], F32)) for i in range(8)]
        s_bank = [bank[0][:, 0:128], bank[0][:, 128:384], bank[1][:, 0:384], bank[2][:, 0:512]]
        t_bank = [bank[3], bank[4]]
        o_bank = bank[5]
        a_bank, b_bank = bank[6], bank[7]

        ld_x0 = sem("ld_x0"); ld_x = sem("ld_x"); ld_w = sem("ld_w"); ld_moe = sem("ld_moe")
        cast_done = sem("cast_done"); pad_ready = sem("pad_ready"); pad_out = sem("pad_out")
        dve_step = sem("dve_step")
        dve_xn = sem("dve_xn"); dve_kT = sem("dve_kT"); dve_vw = sem("dve_vw"); dve_q = sem("dve_q")
        dve_negs = sem("dve_negs"); dve_pn = sem("dve_pn"); dve_x2n = sem("dve_x2n")
        dve_oh = sem("dve_oh"); dve_gap = sem("dve_gap"); dve_slot = sem("dve_slot")
        dve_tab = sem("dve_tab")
        dve_var = [sem("dve_var0"), sem("dve_var1")]; pool_rstd = [sem("pool_rstd0"), sem("pool_rstd1")]
        pe_xnT = sem("pe_xnT"); pe_k = sem("pe_k"); pe_v = sem("pe_v"); pe_vw = sem("pe_vw")
        pe_q = sem("pe_q"); pe_s = sem("pe_s"); pe_t = sem("pe_t"); pe_av = sem("pe_av")
        pe_x2 = sem("pe_x2"); pe_xn2T = sem("pe_xn2T"); pe_lg = sem("pe_lg"); pe_cnt = sem("pe_cnt")
        act_xnT = sem("act_xnT"); act_vT = sem("act_vT"); act_vw = sem("act_vw"); act_p = sem("act_p")
        act_pT = sem("act_pT"); act_oT = sem("act_oT"); act_xn2T = sem("act_xn2T"); act_e2 = sem("act_e2")
        xs_out = sem("xs_out"); rows_free = sem("rows_free"); wd_zero = sem("wd_zero")
        waits_passed = sem("waits_passed")
        fill_out = sem("fill_out")
        xs_in = [sem(f"xs_in{i}") for i in range(NX)]
        y_out = [sem(f"y_out{i}") for i in range(NX)]
        m_xT = sem("m_xT"); m_g = sem("m_g"); m_u = sem("m_u"); m_hT = sem("m_hT"); m_y = sem("m_y")
        m_xTc = sem("m_xTc"); m_sg = sem("m_sg"); m_hid = sem("m_hid"); m_hTc = sem("m_hTc"); m_ys = sem("m_ys")
        y_ld = [sem(f"y_ld{i}") for i in range(B)]
        dve_fin = sem("dve_fin"); out_st = sem("out_st")

        LD_W = 16 * 9
        LD_MOE = 16 * 5

        def passed(engine):
            engine.sem_inc(waits_passed, 1)

        block = ctx.enter_context(nc.Block())

        @block.sync
        def _(sp):
            xv = x.rearrange("b (t p) d -> p (b t) d", p=128)
            xs3 = x_all[:, :].rearrange("p (t d) -> p t d", d=D)
            sp.dma_start(xs3[:, 0:QT, :], xv[:, 0:QT, :]).then_inc(ld_x0, 16)
            for dst, src in ((cst[:, :], consts), (wkv_sb[:, :], wkv), (wq_sb[:, :], wq),
                             (pe_sb[:, :], positions), (bq_sb[:, :], bq),
                             (bkv_sb[:, :], bkv),
                             (wo_sb[:, :].rearrange("p (h n) -> p h n", n=D),
                              wo.rearrange("(h p) n -> p h n", p=D)),
                             (wr_sb[:, :], wr), (dst0[:, :], dest)):
                sp.dma_start(dst, src).then_inc(ld_w, 16)
            for b in range(1, B):
                sp.dma_start(xs3[:, b * QT:(b + 1) * QT, :], xv[:, b * QT:(b + 1) * QT, :]).then_inc(ld_x, 16)
            sp.dma_start(wgu_sb[:, :, 0:I], wg.rearrange("e h i -> h e i")).then_inc(ld_moe, 16)
            sp.dma_start(wgu_sb[:, :, I:2 * I], wu.rearrange("e h i -> h e i")).then_inc(ld_moe, 16)
            for c in range(IC):
                n = min(128, I - c * 128)
                if n < 128:
                    sp.wait_ge(wd_zero, 1)
                sp.dma_start(wd_sb[0:n, :, c, :],
                             wd[:, c * 128:c * 128 + n, :].rearrange("e i n -> i e n")).then_inc(ld_moe, 16)
            sp.wait_ge(pad_ready, 1)
            sp.dma_start(xs_dram[E * CAP:XS_ROWS, :].rearrange("(m p) r -> p m r", p=128),
                         padrows[:, E:PADS, :]).then_inc(pad_out, 16)
            sp.wait_ge(dve_tab, 1)
            for e in range(E):
                row = sp.value_load(fill_i[0:1, e:e + 1], min_val=e * CAP, max_val=e * CAP + NTOK)
                sp.dma_start(xs_dram[bass.ds(row, 128), :], padrows[:, e, :]).then_inc(fill_out, 16)
            sp.wait_ge(dve_tab, 2)
            sp.wait_ge(pad_out, 16)
            sp.wait_ge(fill_out, 16 * E)
            sp.wait_ge(xs_out, 16 * SCATTERS * B)

            def load_group(g, first):
                for i in range(NX):
                    j = g * NX + i
                    row = sp.value_load(row_tab[0:1, bass.ds(j, 1)], min_val=0, max_val=XS_ROWS - 128)
                    if not first:
                        sp.wait_ge(y_out[i], g * 16)
                    sp.dma_start(xs[:, i, :], xs_dram[bass.ds(row, 128), :]).then_inc(xs_in[i], 16)
            load_group(0, True)
            with sp.Fori(1, GROUPS) as g:
                load_group(g, False)
            for i in range(NX):
                sp.wait_ge(y_out[i], 16 * GROUPS)
            for b in range(B):
                for k in range(TOPK):
                    lo = k * NTOK + b * T
                    sp.dma_start(y_in[b][k].rearrange("p (t d) -> p t d", d=D),
                                 y_dram[lo:lo + T, :].rearrange("(t p) d -> p t d", p=128)).then_inc(y_ld[b], 16)
            ov = out.rearrange("b (t p) d -> p (b t) d", p=128)
            for b in range(B):
                sp.wait_ge(dve_fin, b + 1)
                sp.dma_start(ov[:, b * QT:(b + 1) * QT, :], xs3[:, b * QT:(b + 1) * QT, :]).then_inc(out_st, 16)
            sp.wait_ge(out_st, 16 * B)

        @block.gpsimd
        def _(pool):
            def rstds(b, which):
                pool.wait_ge(dve_var[which], b + 1)
                pool.tensor_tensor(rstd[:, which, :], veps[:, which, :], cst[:, C_POW:C_POW + QT],
                                   ALU.pow).then_inc(pool_rstd[which], 1)

            def dispatch(b):
                pool.wait_ge(dve_slot, b + 1)
                if not isinstance(b, int):
                    passed(pool)
                for t in range(QT):
                    for k in range(TOPK):
                        pool.indirect_dma_start(
                            xs_dram[:, :], bass.IndirectOffsetOnAxis(ap=slot[:, k, t:t + 1], axis=0),
                            payload[:, t, k, :], None).then_inc(xs_out, 16)
                pool.wait_ge(xs_out, (b + 1) * (16 * SCATTERS))
                pool.sem_inc(rows_free, 1)

            pool.sem_inc(rows_free, 1)
            pool.wait_ge(ld_w, LD_W)
            rstds(0, 0)
            rstds(1, 0)
            with pool.Fori(1, B - 1) as b:
                rstds(b - 1, 1)
                rstds(b + 1, 0)
                dispatch(b - 1)
            for b in (B - 2, B - 1):
                rstds(b, 1)
                dispatch(b)
            with pool.Fori(0, GROUPS) as g:
                for i in range(NX):
                    pool.wait_ge(m_ys, g * NX + i + 1)
                    passed(pool)
                    pool.indirect_dma_start(
                        y_dram[:, :], bass.IndirectOffsetOnAxis(ap=xs[:, i, D:D + 1].bitcast(I32), axis=0),
                        ys[:, i, :], None).then_inc(y_out[i], 16)

        @block.tensor
        def _(pe):
            def project_x(b, post):
                pe.wait_ge(dve_xn, b + 1)
                if not isinstance(b, int) or b > 0:
                    pe.wait_ge(dve_vw, 4 * b)
                if post is not None:
                    pe.wait_ge(dve_slot, post)
                for t in range(QT):
                    last = pe.transpose(b_bank[:, t * 128:(t + 1) * 128], xn[:, t, :], ident)
                last.then_inc(pe_xnT, 1)

            def project_kv(b):
                pe.wait_ge(act_xnT, b + 1)
                if not isinstance(b, int) or b > 0:
                    pe.wait_ge(dve_q, 8 * b)
                pe.matmul(a_bank[:, :], wkv_sb[:, 0:D], xnT[:, :], start=True, stop=True).then_inc(pe_k, 1)
                pe.matmul(b_bank[:, :], wkv_sb[:, D:2 * D], xnT[:, :], start=True, stop=True).then_inc(pe_v, 1)
                pe.wait_ge(act_vT, b + 1)
                for i in range(2 * QT):
                    if i == 0:
                        pe.wait_ge(dve_kT, b + 1)
                    elif i % 2 == 0:
                        pe.wait_ge(act_vw, 4 * b + i // 2)
                    elif i > 1:
                        pe.wait_ge(dve_vw, 4 * b + i // 2)
                    pe.matmul((a_bank, b_bank)[i % 2][:, :], vT[:, i // 2 * 128:(i // 2 + 1) * 128],
                              wo_sb[:, i % 2 * 512:(i % 2 + 1) * 512], start=True, stop=True).then_inc(pe_vw, 1)

            def queries(b, h):
                if h == 0:
                    pe.wait_ge(act_vw, 4 * b + 4)
                else:
                    pe.wait_ge(dve_q, 8 * b + h)
                pe.matmul(a_bank[:, :], wq_sb[:, h * D:(h + 1) * D], xnT[:, :],
                          start=True, stop=True).then_inc(pe_q, 1)

            def scores(b, h, first):
                pe.wait_ge(dve_q, 8 * b + h + 1)
                for qt in range(QT):
                    n = 32 * b + 4 * h + qt
                    if not (first and h == 0):
                        pe.wait_ge(dve_negs, n - 2 if qt == 0 else n - 3)
                    pe.matmul(s_bank[qt], qT[:, h % 2, qt * 128:(qt + 1) * 128], kT[:, 0:(qt + 1) * 128],
                              start=True, stop=True).then_inc(pe_s, 1)

            def transposes(b, h, first):
                for qt in range(QT):
                    n = 32 * b + 4 * h + qt
                    pe.wait_ge(dve_pn, n + 1)
                    if not (first and h == 0 and qt < 2):
                        pe.wait_ge(act_pT, n - 1)
                    for kt in range(qt + 1):
                        last = pe.transpose(t_bank[qt % 2][:, kt * 128:(kt + 1) * 128],
                                            pr[:, h % 2, qt, kt * 128:(kt + 1) * 128], ident)
                    last.then_inc(pe_t, 1)

            def attend(b, h, first):
                pe.wait_ge(act_pT, 32 * b + 4 * h + 4)
                if h == 0 and not first:
                    pe.wait_ge(act_oT, b)
                for kt in range(QT):
                    last = pe.matmul(o_bank[:, kt * 128:], vw[:, kt, h * D:(h + 1) * D],
                                     pT[:, h % 2, kt, kt * 128:], start=(h == 0 and kt == 0),
                                     stop=(h == H - 1 and kt == QT - 1))
                last.then_inc(pe_av, 1)

            def residual(b, in_body):
                pe.wait_ge(act_oT, b + 1)
                if in_body:
                    pe.wait_ge(dve_vw, 4 * b + 8)
                else:
                    pe.wait_ge(dve_slot, b)
                for t in range(QT):
                    last = pe.transpose(b_bank[:, t * 128:(t + 1) * 128], oT[:, t * 128:(t + 1) * 128], ident)
                last.then_inc(pe_x2, 1)

            def normed(b):
                pe.wait_ge(dve_x2n, b + 1)
                for t in range(QT):
                    last = pe.transpose(b_bank[:, t * 128:(t + 1) * 128], payload[:, t, 0, 0:D], ident)
                last.then_inc(pe_xn2T, 1)

            def logits(b):
                pe.wait_ge(act_xn2T, b + 1)
                for t in range(QT):
                    last = pe.matmul(b_bank[:, t * E:(t + 1) * E], xn2T[:, t * 128:(t + 1) * 128], wr_sb[:, :],
                                     start=True, stop=True)
                last.then_inc(pe_lg, 1)

            def ranks(b):
                pe.wait_ge(dve_oh, b + 1)
                w = QT * E
                pe.matmul(b_bank[:, 64:64 + w], lt_bf[:, :], oh_bf[:, :], start=True, stop=False)
                for t in range(1, QT):
                    pe.matmul(b_bank[:, 64 + t * E:64 + w], one_bf[:, :], oh_bf[:, 0:w - t * E],
                              start=False, stop=(t == QT - 1))
                for t in range(QT):
                    last = pe.matmul(b_bank[:, 128:128 + E], one_bf[:, :], oh_bf[:, t * E:(t + 1) * E],
                                     start=(t == 0), stop=(t == QT - 1))
                last.then_inc(pe_cnt, 1)

            def body(b, first, last):
                for s in range(H + 1):
                    if s < H:
                        scores(b, s, first)
                    if s > 0:
                        transposes(b, s - 1, first)
                    if s + 1 < H:
                        queries(b, s + 1)
                    if s == H and not last:
                        project_x(b + 1, None if first else b)
                    if s > 0:
                        attend(b, s - 1, first)
                    if not first:
                        if s == 0:
                            residual(b - 1, True)
                        if s == 2:
                            normed(b - 1)
                        if s == 3:
                            logits(b - 1)
                        if s == 4:
                            ranks(b - 1)
                if not last:
                    project_kv(b + 1)
                    queries(b + 1, 0)

            pe.wait_ge(ld_w, LD_W)
            project_x(0, None)
            project_kv(0)
            queries(0, 0)
            body(0, True, False)
            with pe.Fori(1, B - 1) as b:
                body(b, False, False)
            body(B - 1, False, True)
            residual(B - 1, False)
            normed(B - 1)
            logits(B - 1)
            ranks(B - 1)

            def m_transpose(g, i):
                j = g * NX + i
                pe.wait_ge(xs_in[i], g * 16 + 16)
                if not (isinstance(g, int) and j < 2):
                    pe.wait_ge(m_xTc, j - 1)
                pe.transpose(bank[i % 2][:, 0:D], xs[:, i, 0:D], ident).then_inc(m_xT, 1)

            def m_gate(g, i, e):
                j = g * NX + i
                pe.wait_ge(m_xTc, j + 1)
                if not (isinstance(g, int) and j < 2):
                    pe.wait_ge(m_sg, j - 1)
                pe.matmul(bank[2 + i % 2][:, 0:I], xsT[:, i % 2, :], wgu_sb[:, bass.ds(e, 1), 0:I],
                          start=True, stop=True).then_inc(m_g, 1)

            def m_up(g, i, e):
                j = g * NX + i
                if not (isinstance(g, int) and j < 2):
                    pe.wait_ge(m_hid, j - 1)
                pe.matmul(bank[4 + i % 2][:, 0:I], xsT[:, i % 2, :], wgu_sb[:, bass.ds(e, 1), I:2 * I],
                          start=True, stop=True).then_inc(m_u, 1)

            def m_hidden_t(g, i):
                j = g * NX + i
                pe.wait_ge(m_hid, j + 1)
                if not (isinstance(g, int) and j < 1):
                    pe.wait_ge(m_hTc, j)
                for c in range(IC):
                    last = pe.transpose(bank[6][:, c * 128:(c + 1) * 128],
                                        hid[:, i % 2, c * 128:(c + 1) * 128], ident)
                last.then_inc(m_hT, 1)

            def m_down(g, i, e):
                j = g * NX + i
                pe.wait_ge(m_hTc, j + 1)
                if not (isinstance(g, int) and j < 1):
                    pe.wait_ge(m_ys, j)
                for c in range(IC):
                    last = pe.matmul(bank[7][:, 0:D], hidT[:, i % 2, c * 128:(c + 1) * 128],
                                     wd_sb[:, bass.ds(e, 1), c, :], start=(c == 0), stop=(c == IC - 1))
                last.then_inc(m_y, 1)

            def expert_group(g, first, last):
                for i in range(NX):
                    gp, ip = (g, i - 1) if i else (g - 1, NX - 1)
                    gn, i_n = (g, i + 1) if i < NX - 1 else (g + 1, 0)
                    e = pe.value_load(e_tab[0:1, bass.ds(g * NX + i, 1)], min_val=0, max_val=E - 1)
                    before = not (first and i == 0)
                    m_gate(g, i, e)
                    if before:
                        m_hidden_t(gp, ip)
                    m_up(g, i, e)
                    if not (last and i == NX - 1):
                        m_transpose(gn, i_n)
                    if before:
                        ep = pe.value_load(e_tab[0:1, bass.ds(g * NX + i - 1, 1)], min_val=0, max_val=E - 1)
                        m_down(gp, ip, ep)

            pe.wait_ge(dve_tab, 2)
            pe.wait_ge(ld_moe, LD_MOE)
            m_transpose(0, 0)
            expert_group(0, True, False)
            with pe.Fori(1, GROUPS - 1) as g:
                expert_group(g, False, False)
            expert_group(GROUPS - 1, False, True)
            m_hidden_t(GROUPS - 1, NX - 1)
            e = pe.value_load(e_tab[0:1, TILES - 1:TILES], min_val=0, max_val=E - 1)
            m_down(GROUPS - 1, NX - 1, e)

        @block.scalar
        def _(act):
            def project_x(b):
                act.wait_ge(pe_xnT, b + 1)
                act.copy(xnT[:, :], b_bank[:, :]).then_inc(act_xnT, 1)

            def project_kv(b):
                act.wait_ge(pe_v, b + 1)
                act.activation(vT[:, :], b_bank[:, :], ACT.Identity, bias=bkv_sb[:, 1:2]).then_inc(act_vT, 1)
                for i in range(QT):
                    act.wait_ge(pe_vw, 8 * b + 2 * i + 1)
                    if i == 0 and (not isinstance(b, int) or b > 0):
                        act.wait_ge(pe_av, 8 * b)
                    act.copy(vw[:, i, 0:512], a_bank[:, :]).then_inc(act_vw, 1)

            def exps(b, h, qt, first):
                n = 32 * b + 4 * h + qt
                act.wait_ge(dve_negs, n + 1)
                if not (first and h < 2):
                    act.wait_ge(pe_t, n - 7)
                w = (qt + 1) * 128
                act.activation(pr[:, h % 2, qt, 0:w], negs[:, qt, 0:w], ACT.Exp,
                               bias=nmax[:, h % 2, qt:qt + 1], scale=-1.0,
                               accum_out=rsum[:, h % 2, qt:qt + 1]).then_inc(act_p, 1)

            def evacuate(b, h, qt, first):
                act.wait_ge(pe_t, 32 * b + 4 * h + qt + 1)
                if qt == 0 and not (first and h < 2):
                    act.wait_ge(pe_av, 8 * b + h - 1)
                act.copy(pT[:, h % 2, 0:qt + 1, qt * 128:(qt + 1) * 128],
                         t_bank[qt % 2][:, 0:(qt + 1) * 128].rearrange("p (k q) -> p k q", q=128)).then_inc(act_pT, 1)

            def body(b, first, last):
                for s in range(H + 1):
                    if s == 3 and not first:
                        act.wait_ge(pe_xn2T, b)
                        act.copy(xn2T[:, :], b_bank[:, :]).then_inc(act_xn2T, 1)
                    if s == 5 and not first:
                        act.wait_ge(dve_gap, b)
                        act.activation(e2[:, :], gap[:, :], ACT.Exp).then_inc(act_e2, 1)
                    for qt in range(QT):
                        if s < H:
                            exps(b, s, qt, first)
                        if s > 0 and qt > 0:
                            evacuate(b, s - 1, qt - 1, first)
                    if s > 0:
                        evacuate(b, s - 1, QT - 1, first)
                if not last:
                    project_x(b + 1)
                act.wait_ge(pe_av, 8 * b + 8)
                if not first:
                    act.wait_ge(pe_x2, b)
                act.copy(oT[:, :], o_bank[:, :]).then_inc(act_oT, 1)
                if not last:
                    project_kv(b + 1)

            act.wait_ge(ld_w, LD_W)
            project_x(0)
            project_kv(0)
            body(0, True, False)
            with act.Fori(1, B - 1) as b:
                body(b, False, False)
            body(B - 1, False, True)
            act.wait_ge(pe_xn2T, B)
            act.copy(xn2T[:, :], b_bank[:, :]).then_inc(act_xn2T, 1)
            act.wait_ge(dve_gap, B)
            act.activation(e2[:, :], gap[:, :], ACT.Exp).then_inc(act_e2, 1)

            def m_rows(g, i):
                j = g * NX + i
                act.wait_ge(m_xT, j + 1)
                if not (isinstance(g, int) and j < 2):
                    act.wait_ge(m_u, j - 1)
                act.copy(xsT[:, i % 2, :], bank[i % 2][:, 0:D]).then_inc(m_xTc, 1)

            def m_silu(g, i):
                j = g * NX + i
                act.wait_ge(m_g, j + 1)
                if not (isinstance(g, int) and j < 2):
                    act.wait_ge(m_hid, j - 1)
                act.activation(sg[:, i % 2, :], bank[2 + i % 2][:, 0:I], ACT.Silu).then_inc(m_sg, 1)

            def m_result(g, i):
                j = g * NX + i
                act.wait_ge(m_y, j + 1)
                if not (isinstance(g, int) and g < 1):
                    act.wait_ge(y_out[i], g * 16)
                act.activation(ys[:, i, :], bank[7][:, 0:D], ACT.Copy,
                               scale=xs[:, i, D + 1:D + 2]).then_inc(m_ys, 1)

            def expert_group(g, first, last):
                for i in range(NX):
                    m_silu(g, i)
                    if not (last and i == NX - 1):
                        m_rows(*((g, i + 1) if i < NX - 1 else (g + 1, 0)))
                    if not (first and i == 0):
                        m_result(*((g, i - 1) if i else (g - 1, NX - 1)))

            m_rows(0, 0)
            expert_group(0, True, False)
            with act.Fori(1, GROUPS - 1) as g:
                expert_group(g, False, False)
            expert_group(GROUPS - 1, False, True)
            m_result(GROUPS - 1, NX - 1)

        @block.vector
        def _(dve):
            count = {"base": 0, "n": 0}

            def link(ins):
                count["n"] += 1
                ins.then_inc(dve_step, 1)
                dve.wait_ge(dve_step, count["base"] + count["n"])

            def layer_norm(b, which, src, st_, mv_, write):
                if not isinstance(b, int):
                    passed(dve)
                for t in range(QT):
                    ins = dve.bn_stats(st_[:, t, :], src(t))
                link(ins)
                if not isinstance(b, int):
                    passed(dve)
                for t in range(QT):
                    ins = dve.bn_aggr(mv_[:, t, :], st_[:, t, :])
                link(ins)
                dve.tensor_scalar(veps[:, which, :], mv_[:, :, 1], EPS, None, ALU.add).then_inc(dve_var[which], 1)
                dve.wait_ge(pool_rstd[which], b + 1)
                for t in range(QT):
                    ins = write(t, src(t), mv_[:, t, 0:1], rstd[:, which, t:t + 1])
                return ins

            def norm_in(b):
                def write(t, tile, m, r):
                    return dve.tensor_scalar(xn[:, t, :], tile, m, r, ALU.subtract, ALU.mult)
                if not isinstance(b, int) or b > 0:
                    dve.wait_ge(pe_xnT, b)
                layer_norm(b, 0, lambda t: x_all[:, bass.ds(b * T + t * D, D)], stats, mv, write).then_inc(dve_xn, 1)

            def project_kv(b):
                dve.wait_ge(pe_k, b + 1)
                if not isinstance(b, int) or b > 0:
                    dve.wait_ge(pe_s, 32 * b)
                dve.scalar_tensor_tensor(out=kT[:, :], in0=a_bank[:, :], scalar=bkv_sb[:, 0:1], in1=pe_sb[:, :],
                                         op0=ALU.add, op1=ALU.add).then_inc(dve_kT, 1)
                for i in range(QT):
                    dve.wait_ge(pe_vw, 8 * b + 2 * i + 2)
                    if i == 0 and (not isinstance(b, int) or b > 0):
                        dve.wait_ge(pe_av, 8 * b)
                    dve.tensor_copy(vw[:, i, 512:1024], b_bank[:, :]).then_inc(dve_vw, 1)

            def queries(b, h, first):
                dve.wait_ge(pe_q, 8 * b + h + 1)
                if not (first and h < 2):
                    dve.wait_ge(pe_s, 32 * b + 4 * h - 4)
                dve.scalar_tensor_tensor(out=qT[:, h % 2, :], in0=a_bank[:, :], scalar=bq_sb[:, h:h + 1],
                                         in1=pe_sb[:, :], op0=ALU.add, op1=ALU.add).then_inc(dve_q, 1)

            def masked(b, h):
                for qt in range(QT):
                    n = 32 * b + 4 * h + qt
                    dve.wait_ge(pe_s, n + (2 if qt == 0 else 1))
                    w = (qt + 1) * 128
                    if not isinstance(b, int):
                        passed(dve)
                    dve.tensor_tensor_reduce(out=negs[:, qt, 0:w], in0=s_bank[qt],
                                             in1=cst[:, C_MASK + T - w:C_MASK + T], scale=-SCALE, scalar=BIG,
                                             op0=ALU.add, op1=ALU.min,
                                             accum_out=nmax[:, h % 2, qt:qt + 1]).then_inc(dve_negs, 1)

            def normalise(b, h):
                for qt in range(QT):
                    dve.wait_ge(act_p, 32 * b + 4 * h + qt + 1)
                    link(dve.reciprocal(rinv[:, h % 2, qt:qt + 1], rsum[:, h % 2, qt:qt + 1]))
                    w = (qt + 1) * 128
                    dve.tensor_scalar(pr[:, h % 2, qt, 0:w], pr[:, h % 2, qt, 0:w], rinv[:, h % 2, qt:qt + 1],
                                      None, ALU.mult).then_inc(dve_pn, 1)

            def residual(b):
                dve.wait_ge(pe_x2, b + 1)
                xb = x_all[:, bass.ds(b * T, T)]
                link(dve.tensor_tensor(xb, b_bank[:, :], xb, ALU.add))
                dve.wait_ge(rows_free, b + 1)

                def write(t, tile, m, r):
                    return dve.tensor_scalar(payload[:, t, :, 0:D],
                                             tile.rearrange("p (o d) -> p o d", o=1).broadcast_to((128, TOPK, D)),
                                             m, r, ALU.subtract, ALU.mult)
                layer_norm(b, 1, lambda t: x_all[:, bass.ds(b * T + t * D, D)], stats2, mv2, write)
                d = payload[:, :, :, D].bitcast(I32)
                dve.tensor_scalar(d, d, T, None, ALU.add).then_inc(dve_x2n, 1)

            def e3(ap):
                return ap.rearrange("p (t e) -> p t e", e=E)

            def b3(ap):
                return ap.rearrange("p (t o) -> p t o", o=1).broadcast_to((128, QT, E))

            def choose(b):
                dve.wait_ge(pe_lg, b + 1)
                link(dve.tensor_copy(lg[:, 0, :], b_bank[:, 0:QT * E]))
                for k in range(TOPK):
                    link(dve.reduce_max(top[:, k, :], e3(lg[:, k, :]), AX.X))
                    link(dve.tensor_tensor(e3(iseq[:, :]), e3(lg[:, k, :]), b3(top[:, k, :]), ALU.is_ge))
                    link(dve.tensor_tensor(key[:, :], iseq[:, :], cst[:, C_REV:C_REV + QT * E], ALU.mult))
                    link(dve.reduce_max(kmax[:, :], e3(key[:, :]), AX.X))
                    link(dve.tensor_tensor(e3(oh[:, k, :]), e3(key[:, :]), b3(kmax[:, :]), ALU.is_equal))
                    if k == 0:
                        link(dve.scalar_tensor_tensor(out=lg[:, 1, :], in0=oh[:, 0, :], scalar=-BIG,
                                                      in1=lg[:, 0, :], op0=ALU.mult, op1=ALU.add))
                dve.tensor_tensor(oh_bf[:, :], oh[:, 0, :], oh[:, 1, :], ALU.add).then_inc(dve_oh, 1)
                dve.tensor_tensor(gap[:, :], top[:, 1, :], top[:, 0, :], ALU.subtract).then_inc(dve_gap, 1)

            def place(b):
                dve.wait_ge(act_e2, b + 1)
                link(dve.tensor_scalar(den[:, :], e2[:, :], 1.0, None, ALU.add))
                link(dve.reciprocal(wrow[:, :, 0], den[:, :]))
                link(dve.tensor_tensor(wrow[:, :, 1], e2[:, :], wrow[:, :, 0], ALU.mult))
                dve.tensor_copy(payload[:, :, :, D + 1], wrow[:, :, :])
                dve.wait_ge(pe_cnt, b + 1)
                link(dve.tensor_tensor(
                    e3(pos[:, :]), e3(b_bank[:, 64:64 + QT * E]),
                    fill[:, :].rearrange("p (o e) -> p o e", o=1).broadcast_to((128, QT, E)), ALU.add))
                for k in range(TOPK):
                    link(dve.tensor_tensor(posk[:, k, :], oh[:, k, :], pos[:, :], ALU.mult))
                    link(dve.reduce_sum(slot_f[:, k, :], e3(posk[:, k, :]), AX.X))
                link(dve.tensor_tensor(fill[:, :], fill[:, :], b_bank[:, 128:128 + E], ALU.add))
                dve.tensor_copy(slot[:, :, :], slot_f[:, :, :]).then_inc(dve_slot, 1)

            def body(b, first, last):
                at = count["n"]
                for s in range(H + 1):
                    if s < H:
                        masked(b, s)
                        normalise(b, s)
                    if s + 1 < H:
                        queries(b, s + 1, first)
                    if s == 4 and not last:
                        norm_in(b + 1)
                    if not first:
                        if s == 1:
                            residual(b - 1)
                        if s == 4:
                            choose(b - 1)
                        if s == 5:
                            place(b - 1)
                if not last:
                    project_kv(b + 1)
                    queries(b + 1, 0, False)
                assert first or last or count["n"] - at == STEPS

            dve.wait_ge(ld_x0, 16)
            norm_in(0)
            dve.memset(wd_sb[96:128, :, IC - 1, :], 0.0).then_inc(wd_zero, 1)
            dve.memset(hid[:, :, I:IP], 0.0)
            link(dve.memset(padrows[:, :, :], 0.0))
            dve.wait_ge(ld_w, LD_W)
            project_kv(0)
            queries(0, 0, True)
            dve.tensor_copy(lt_bf[:, :], cst[:, C_LT:C_LT + 128])
            dve.tensor_copy(one_bf[:, :], cst[:, C_ONE:C_ONE + 128]).then_inc(cast_done, 1)
            dve.tensor_copy(fill[:, :], cst[:, C_CAP:C_CAP + E])
            link(dve.tensor_copy(payload[:, :, :, D].bitcast(I32),
                                 dst0[:, 0:SCATTERS].rearrange("p (t k) -> p t k", k=TOPK)))
            dve.tensor_copy(padrows[:, :, D].bitcast(I32), dst0[:, SCATTERS:]).then_inc(pad_ready, 1)
            dve.wait_ge(ld_x, 16 * (B - 1))
            body(0, True, False)
            count["base"], count["n"] = count["n"], 0
            before = count["base"]
            with dve.Fori(1, B - 1) as b:
                count["base"], count["n"] = (b - 1) * STEPS + before, 0
                body(b, False, False)
            count["base"], count["n"] = before + (B - 2) * STEPS, 0
            body(B - 1, False, True)
            residual(B - 1)
            choose(B - 1)
            place(B - 1)

            dve.tensor_copy(fill_i[:, :], fill[:, :]).then_inc(dve_tab, 1)
            link(dve.tensor_tensor(cnt[:, :], fill[:, :], cst[:, C_CAP:C_CAP + E], ALU.subtract))

            def wide(ap, n):
                return ap.rearrange("p (m o) -> p m o", o=1).broadcast_to((128, ap.shape[1], n))

            def tall(ap, n):
                return ap.rearrange("p (o m) -> p o m", o=1).broadcast_to((128, n, ap.shape[1]))

            link(dve.tensor_tensor(over[:, :].rearrange("p (e m) -> p e m", m=NT), wide(cnt[:, :], NT),
                                   tall(cst[:, C_THR:C_THR + NT], E), ALU.is_gt))
            link(dve.reduce_sum(ntile[:, :], over[:, :].rearrange("p (e m) -> p e m", m=NT), AX.X))
            link(dve.tensor_tensor(cumm[:, :].rearrange("p (e f) -> p e f", f=E),
                                   cst[:, C_LE:C_LE + E * E].rearrange("p (e f) -> p e f", f=E),
                                   tall(ntile[:, :], E), ALU.mult))
            link(dve.reduce_sum(cum[:, :], cumm[:, :].rearrange("p (e f) -> p e f", f=E), AX.X))
            j3 = done[:, :].rearrange("p (j e) -> p j e", e=E)
            k3 = skip[:, :].rearrange("p (j e) -> p j e", e=E)
            link(dve.tensor_tensor(j3, tall(cum[:, :], TILES), wide(cst[:, C_J:C_J + TILES], E), ALU.is_le))
            link(dve.reduce_sum(ej[:, :], j3, AX.X))
            link(dve.tensor_tensor(k3, j3, tall(ntile[:, :], TILES), ALU.mult))
            link(dve.reduce_sum(st[:, :], k3, AX.X))
            link(dve.tensor_tensor(st[:, :], cst[:, C_J:C_J + TILES], st[:, :], ALU.subtract))
            link(dve.tensor_scalar(st[:, :], st[:, :], 128.0, None, ALU.mult))
            link(dve.scalar_tensor_tensor(out=rowf[:, :], in0=ej[:, :], scalar=float(CAP), in1=st[:, :],
                                          op0=ALU.mult, op1=ALU.add))
            dve.tensor_copy(row_tab[:, :], rowf[:, :])
            dve.tensor_scalar(e_tab[:, :], ej[:, :], float(E - 1), None, ALU.min).then_inc(dve_tab, 1)

            def m_hidden(g, i):
                j = g * NX + i
                dve.wait_ge(m_sg, j + 1)
                dve.wait_ge(m_u, j + 1)
                if not (isinstance(g, int) and j < 2):
                    dve.wait_ge(m_hT, j - 1)
                dve.tensor_tensor(hid[:, i % 2, 0:I], sg[:, i % 2, :], bank[4 + i % 2][:, 0:I],
                                  ALU.mult).then_inc(m_hid, 1)

            def m_hidden_t(g, i):
                j = g * NX + i
                dve.wait_ge(m_hT, j + 1)
                if not (isinstance(g, int) and j < 2):
                    dve.wait_ge(m_y, j - 1)
                dve.tensor_copy(hidT[:, i % 2, :], bank[6][:, 0:IP]).then_inc(m_hTc, 1)

            def expert_group(g, first):
                for i in range(NX):
                    if not (first and i == 0):
                        m_hidden_t(*((g, i - 1) if i else (g - 1, NX - 1)))
                    m_hidden(g, i)

            expert_group(0, True)
            with dve.Fori(1, GROUPS) as g:
                expert_group(g, False)
            m_hidden_t(GROUPS - 1, NX - 1)

            for b in range(B):
                dve.wait_ge(y_ld[b], 16 * TOPK)
                xb = x_all[:, b * T:(b + 1) * T]
                link(dve.tensor_tensor(xb, xb, y_in[b][0], ALU.add))
                dve.tensor_tensor(xb, xb, y_in[b][1], ALU.add).then_inc(dve_fin, 1)


INPUTS = ("L0_attn_x", "L0_attn_Wq", "L0_attn_bq", "L0_attn_Wkv", "L0_attn_bkv", "L0_attn_Wo",
          "L0_ffn_Wr", "L0_ffn_Wg", "L0_ffn_Wu", "L0_ffn_Wd")


def kernel(**inputs):
    import concourse.bacc as bacc
    from concourse.bass_utils import run_bass_kernel_spmd

    nc = bacc.Bacc("TRN2", target_bir_lowering=False, num_devices=1)
    given = [(n, np.ascontiguousarray(inputs[n])) for n in INPUTS]
    given += list(zip(("consts", "dest", "positions"), constants()))
    given = [(n, np.ascontiguousarray(a.reshape(-1, D).T) if n in ("L0_attn_bq", "L0_attn_bkv") else a)
             for n, a in given]
    arrays, args = {}, []
    for name, a in given:
        arrays[name] = a
        args.append(nc.dram_tensor(name, a.shape, mybir.dt.from_np(a.dtype), kind="ExternalInput").ap())
    out = nc.dram_tensor("out", (B, T, D), F32, kind="ExternalOutput").ap()
    block_kernel(nc, *args, out)
    r = run_bass_kernel_spmd(nc, [arrays], core_ids=[0])
    return r.results[0]["out"]
```

```python
from contextlib import ExitStack

import numpy as np

import concourse.bass as bass
from concourse import mybir

F32, F32R = mybir.dt.float32, mybir.dt.float32r
BF16, I32 = mybir.dt.bfloat16, mybir.dt.int32
ALU = mybir.AluOpType
ACT = mybir.ActivationFunctionType
AX = mybir.AxisListType

B, T, D = 8, 512, 128
H = 8
QT = T // 128
NTOK = B * T
NT = NTOK // 128
E, I, TOPK = 9, 352, 2
IC = 3
IP = IC * 128
SCALE = float(D) ** -0.5
EPS = 1e-5
NEG = -1.0e30
BIG = 3.0e38

ROW = D + 2
CAP = NTOK + 128
NX = 8
TILES = -(-(TOPK * NTOK // 128 + E - 1) // NX) * NX
SPARE = TILES - TOPK * NTOK // 128
PADS = E + SPARE
XS_ROWS = E * CAP + SPARE * 128
Y_ROWS = TOPK * NTOK + PADS * 128
SCATTERS = QT * TOPK
GROUPS = TILES // NX
PR = [128 * (qt * (qt + 1) // 2) for qt in range(QT + 1)]

STEPS = 2 * H + 2 * 2 + 1 + (5 * TOPK + 1) + (3 + 1 + 2 * TOPK + 1)

C_ID = 0
C_MASK = C_ID + 128
C_LT = C_MASK + T
C_ONE = C_LT + 128
C_REV = C_ONE + 128
C_THR = C_REV + QT * E
C_LE = C_THR + NT
C_J = C_LE + E * E
C_CAP = C_J + TILES
C_POW = C_CAP + E
C_END = C_POW + QT


def constants():
    c = np.zeros((128, C_END), np.float32)
    p = np.arange(128)
    c[:, C_ID:C_ID + 128] = np.eye(128)
    c[:, C_MASK + T - 128:C_MASK + T] = np.where(p[None, :] > p[:, None], NEG, 0.0)
    c[:, C_LT:C_LT + 128] = p[:, None] < p[None, :]
    c[:, C_ONE:C_ONE + 128] = 1.0
    c[:, C_REV:C_REV + QT * E] = np.tile(E - np.arange(E), QT)
    c[:, C_THR:C_THR + NT] = 128 * np.arange(NT)
    c[:, C_LE:C_LE + E * E] = (np.arange(E)[None, :] <= np.arange(E)[:, None]).reshape(-1)
    c[:, C_J:C_J + TILES] = np.arange(TILES)
    c[:, C_CAP:C_CAP + E] = CAP * np.arange(E)
    c[:, C_POW:C_POW + QT] = -0.5
    t, k = np.arange(QT)[:, None], np.arange(TOPK)[None, :]
    pairs = (k * NTOK + t * 128 - T).reshape(1, -1) + p[:, None]
    pads = TOPK * NTOK + 128 * np.arange(PADS)[None, :] + p[:, None]
    dest = np.concatenate([pairs, pads], 1).astype(np.int32)
    pos = np.arange(T, dtype=np.float32)[:, None]
    inv = np.exp(np.float32(-np.log(10000.0)) * np.arange(0, D, 2, dtype=np.float32) / np.float32(D))
    ang = pos * inv[None, :].astype(np.float32)
    pe = np.zeros((T, D), np.float32)
    pe[:, 0::2] = np.sin(ang)
    pe[:, 1::2] = np.cos(ang)
    return c, dest, np.ascontiguousarray(pe.T)


def block_kernel(nc, x, wq, bq, wkv, bkv, wo, wr, wg, wu, wd, consts, dest, positions, out):
    ctx = ExitStack()
    with ctx:
        def sb(name, shape, dt=F32):
            return ctx.enter_context(nc.sbuf_tensor(name, shape, dt))

        def sem(name):
            return ctx.enter_context(nc.semaphore(name))

        xs_dram = nc.dram_tensor("xs_dram", (XS_ROWS, ROW), F32, kind="Internal").ap()
        y_dram = nc.dram_tensor("y_dram", (Y_ROWS, D), F32, kind="Internal").ap()

        cst = sb("cst", [128, C_END])
        dst0 = sb("dst0", [128, SCATTERS + PADS], I32)
        pe_sb = sb("pe_sb", [128, T])
        wq_sb = [sb(f"wq_sb{i}", [128, H * D], F32R) for i in range(2)]
        wkv_sb = [sb(f"wkv_sb{i}", [128, 2 * D], F32R) for i in range(2)]
        wo_sb = [sb(f"wo_sb{i}", [128, H * D], F32R) for i in range(2)]
        wr_sb = sb("wr_sb", [128, E])
        bq_sb = sb("bq_sb", [128, H])
        bkv_sb = sb("bkv_sb", [128, 2])
        wgu_sb = [sb(f"wgu_sb{i}", [128, E, 2 * I], F32R) for i in range(2)]
        wgu_in = sb("wgu_in", [128, 2, 2 * I])
        wd_sb = sb("wd_sb", [128, E, IC, D])
        lt_bf = sb("lt_bf", [128, 128], BF16)
        one_bf = sb("one_bf", [128, 128], BF16)
        ident = cst[:, C_ID:C_ID + 128]

        x_all = sb("x_all", [128, NT * D])
        stats = sb("stats", [128, QT, 6])
        mv = sb("mv", [128, QT, 2])
        veps = sb("veps", [128, 2, QT])
        rstd = sb("rstd", [128, 2, QT])
        xn = sb("xn", [128, QT, D])
        xnT = [sb(f"xnT{i}", [128, T], F32R) for i in range(2)]
        kT_in = sb("kT_in", [128, 2, T])
        kT = [sb(f"kT{i}", [128, 2, T], F32R) for i in range(2)]
        vT = [sb(f"vT{i}", [128, T], F32R) for i in range(2)]
        vw = sb("vw", [128, QT, H * D])
        qT_in = sb("qT_in", [128, 2, T])
        qT = [sb(f"qT{i}", [128, 2, T], F32R) for i in range(2)]
        nmax = sb("nmax", [128, 2, QT])
        rsum = sb("rsum", [128, 2, QT])
        rinv = sb("rinv", [128, 2, QT])
        pr = sb("pr", [128, 2, PR[QT]])
        pT = sb("pT", [128, 2, QT, T])
        oT = sb("oT", [128, T])

        payload = sb("payload", [128, QT, TOPK, ROW])
        stats2 = sb("stats2", [128, QT, 6])
        mv2 = sb("mv2", [128, QT, 2])
        xn2T = oT
        lg = sb("lg", [128, TOPK, QT * E])
        top = sb("top", [128, TOPK, QT])
        iseq = sb("iseq", [128, QT * E])
        key = sb("key", [128, QT * E])
        kmax = sb("kmax", [128, QT])
        oh = sb("oh", [128, TOPK, QT * E])
        oh_bf = sb("oh_bf", [128, QT * E], BF16)
        gap = sb("gap", [128, QT])
        e2 = sb("e2", [128, QT])
        den = sb("den", [128, QT])
        wrow = sb("wrow", [128, QT, TOPK])
        pos = sb("pos", [128, QT * E])
        posk = sb("posk", [128, TOPK, QT * E])
        slot_f = sb("slot_f", [128, TOPK, QT])
        slot = sb("slot", [128, TOPK, QT], I32)
        fill = sb("fill", [128, E])
        padrows = sb("padrows", [128, PADS, ROW])
        cnt = sb("cnt", [128, E])
        over = sb("over", [128, E * NT])
        ntile = sb("ntile", [128, E])
        cumm = sb("cumm", [128, E * E])
        cum = sb("cum", [128, E])
        ej = sb("ej", [128, TILES])
        st = sb("st", [128, TILES])
        rowf = sb("rowf", [128, TILES])
        row_tab = sb("row_tab", [128, TILES], I32)
        e_tab = sb("e_tab", [128, TILES], I32)
        fill_i = sb("fill_i", [128, E], I32)

        pr_flat = pr[:, :, :].rearrange("p a n -> p (a n)")
        pT_flat = pT[:, :, :, :].rearrange("p a k n -> p (a k n)")

        def carve(flat, shapes):
            at, views = 0, []
            for a, n in shapes:
                v = flat[:, at:at + a * n]
                views.append(v.rearrange("p (a n) -> p a n", n=n) if a > 1 else v)
                at += a * n
            return views
        xs, ys = carve(pr_flat, [(NX, ROW), (NX, D)])
        sg, hid, hidT, done, skip = carve(pT_flat, [(2, I), (2, IP), (2, IP), (1, TILES * E), (1, TILES * E)])
        xsT = [sb(f"xsT{i}", [128, 2, D], F32R) for i in range(2)]
        wq_in, wkv_in, wo_in = carve(pT_flat, [(1, H * D), (1, 2 * D), (1, H * D)])
        vw_flat = vw[:, :, :].rearrange("p k n -> p (k n)")
        y_in = [[f[:, b * T:(b + 1) * T] for f in (pT_flat, vw_flat)] for b in range(B)]

        bank = [ctx.enter_context(nc.psum_tensor(f"bank{i}", [128, 512], F32)) for i in range(8)]
        s_bank = [bank[0][:, 0:128], bank[0][:, 128:384], bank[1][:, 0:384], bank[2][:, 0:512]]
        t_bank = [bank[3], bank[4]]
        o_bank = bank[5]
        a_bank, b_bank = bank[6], bank[7]

        ld_x0 = sem("ld_x0"); ld_x = sem("ld_x"); ld_w = sem("ld_w"); ld_moe = sem("ld_moe")
        cast_done = sem("cast_done"); pad_ready = sem("pad_ready"); pad_out = sem("pad_out")
        dve_step = sem("dve_step")
        act_whi = sem("act_whi"); dve_wlo = sem("dve_wlo"); ld_gu = [sem("ld_gu0"), sem("ld_gu1")]
        pool_gu = sem("pool_gu"); act_qh = sem("act_qh"); pool_ql = sem("pool_ql"); act_kh = sem("act_kh")
        dve_kl = sem("dve_kl"); pool_step = sem("pool_step"); dve_vl = sem("dve_vl"); dve_xl = sem("dve_xl"); m_xTl = sem("m_xTl")
        dve_xn = sem("dve_xn"); dve_kT = sem("dve_kT"); dve_vw = sem("dve_vw"); dve_q = sem("dve_q")
        dve_negs = sem("dve_negs"); dve_pn = sem("dve_pn"); dve_x2n = sem("dve_x2n")
        dve_oh = sem("dve_oh"); dve_gap = sem("dve_gap"); dve_slot = sem("dve_slot"); dve_lg = sem("dve_lg")
        dve_tab = sem("dve_tab")
        dve_var = [sem("dve_var0"), sem("dve_var1")]; pool_rstd = [sem("pool_rstd0"), sem("pool_rstd1")]
        pe_xnT = sem("pe_xnT"); pe_k = sem("pe_k"); pe_v = sem("pe_v"); pe_vw = sem("pe_vw")
        pe_q = sem("pe_q"); pe_s = sem("pe_s"); pe_t = sem("pe_t"); pe_av = sem("pe_av")
        pe_x2 = sem("pe_x2"); pe_xn2T = sem("pe_xn2T"); pe_lg = sem("pe_lg"); pe_cnt = sem("pe_cnt")
        act_xnT = sem("act_xnT"); act_vT = sem("act_vT"); act_vw = sem("act_vw"); act_p = sem("act_p")
        act_pT = sem("act_pT"); act_oT = sem("act_oT"); act_xn2T = sem("act_xn2T"); act_e2 = sem("act_e2")
        xs_out = sem("xs_out"); rows_free = sem("rows_free"); wd_zero = sem("wd_zero")
        waits_passed = sem("waits_passed")
        fill_out = sem("fill_out")
        xs_in = [sem(f"xs_in{i}") for i in range(NX)]
        y_out = [sem(f"y_out{i}") for i in range(NX)]
        m_xT = sem("m_xT"); m_g = sem("m_g"); m_u = sem("m_u"); m_hT = sem("m_hT"); m_y = sem("m_y")
        m_xTc = sem("m_xTc"); m_sg = sem("m_sg"); m_hid = sem("m_hid"); m_hTc = sem("m_hTc"); m_ys = sem("m_ys")
        y_ld = [sem(f"y_ld{i}") for i in range(B)]
        dve_fin = sem("dve_fin"); out_st = sem("out_st")

        LD_W = 16 * 9
        LD_MOE = 16 * IC

        def passed(engine):
            engine.sem_inc(waits_passed, 1)

        block = ctx.enter_context(nc.Block())

        @block.sync
        def _(sp):
            xv = x.rearrange("b (t p) d -> p (b t) d", p=128)
            xs3 = x_all[:, :].rearrange("p (t d) -> p t d", d=D)
            sp.dma_start(xs3[:, 0:QT, :], xv[:, 0:QT, :]).then_inc(ld_x0, 16)
            for dst, src in ((cst[:, :], consts), (wkv_in, wkv), (wq_in, wq),
                             (pe_sb[:, :], positions), (bq_sb[:, :], bq),
                             (bkv_sb[:, :], bkv),
                             (wo_in.rearrange("p (h n) -> p h n", n=D),
                              wo.rearrange("(h p) n -> p h n", p=D)),
                             (wr_sb[:, :], wr), (dst0[:, :], dest)):
                sp.dma_start(dst, src).then_inc(ld_w, 16)
            for b in range(1, B):
                sp.dma_start(xs3[:, b * QT:(b + 1) * QT, :], xv[:, b * QT:(b + 1) * QT, :]).then_inc(ld_x, 16)
            for e in range(E):
                if e > 1:
                    sp.wait_ge(pool_gu, e - 1)
                for k, w in enumerate((wg, wu)):
                    sp.dma_start(wgu_in[:, e % 2, k * I:(k + 1) * I], w[e, :, :]).then_inc(ld_gu[e % 2], 16)
            for c in range(IC):
                n = min(128, I - c * 128)
                if n < 128:
                    sp.wait_ge(wd_zero, 1)
                sp.dma_start(wd_sb[0:n, :, c, :],
                             wd[:, c * 128:c * 128 + n, :].rearrange("e i n -> i e n")).then_inc(ld_moe, 16)
            sp.wait_ge(pad_ready, 1)
            sp.dma_start(xs_dram[E * CAP:XS_ROWS, :].rearrange("(m p) r -> p m r", p=128),
                         padrows[:, E:PADS, :]).then_inc(pad_out, 16)
            sp.wait_ge(dve_tab, 1)
            for e in range(E):
                row = sp.value_load(fill_i[0:1, e:e + 1], min_val=e * CAP, max_val=e * CAP + NTOK)
                sp.dma_start(xs_dram[bass.ds(row, 128), :], padrows[:, e, :]).then_inc(fill_out, 16)
            sp.wait_ge(dve_tab, 2)

            def load_group(g, first):
                rows = []
                for i in range(0, NX, 4):
                    rows += nc.values_load_multi_w_load_instructions(
                        row_tab[0:1, bass.ds(g * NX + i, 4)], engines=(mybir.EngineType.SP,), min_val=0,
                        max_val=XS_ROWS - 128, skip_runtime_bounds_check_because="made of counts of tokens")[1]
                if first:
                    sp.wait_ge(pad_out, 16)
                    sp.wait_ge(fill_out, 16 * E)
                    sp.wait_ge(xs_out, 16 * SCATTERS * B)
                for i in range(NX):
                    if not first:
                        sp.wait_ge(y_out[i], g * 16)
                    sp.dma_start(xs[:, i, :], xs_dram[bass.ds(rows[i], 128), :]).then_inc(xs_in[i], 16)
            load_group(0, True)
            with sp.Fori(1, GROUPS) as g:
                load_group(g, False)
            for i in range(NX):
                sp.wait_ge(y_out[i], 16 * GROUPS)
            for b in range(B):
                for k in range(TOPK):
                    lo = k * NTOK + b * T
                    sp.dma_start(y_in[b][k].rearrange("p (t d) -> p t d", d=D),
                                 y_dram[lo:lo + T, :].rearrange("(t p) d -> p t d", p=128)).then_inc(y_ld[b], 16)
            ov = out.rearrange("b (t p) d -> p (b t) d", p=128)
            for b in range(B):
                sp.wait_ge(dve_fin, b + 1)
                sp.dma_start(ov[:, b * QT:(b + 1) * QT, :], xs3[:, b * QT:(b + 1) * QT, :]).then_inc(out_st, 16)
            sp.wait_ge(out_st, 16 * B)

        @block.gpsimd
        def _(pool):
            def rstds(b, which):
                pool.wait_ge(dve_var[which], b + 1)
                pool.tensor_tensor(rstd[:, which, :], veps[:, which, :], cst[:, C_POW:C_POW + QT],
                                   ALU.pow).then_inc(pool_rstd[which], 1)

            def dispatch(b, n, m):
                if n == 0:
                    pool.wait_ge(dve_slot, b + 1)
                    if not isinstance(b, int):
                        passed(pool)
                for i in range(n, m):
                    t, k = i // TOPK, i % TOPK
                    pool.indirect_dma_start(
                        xs_dram[:, :], bass.IndirectOffsetOnAxis(ap=slot[:, k, t:t + 1], axis=0),
                        payload[:, t, k, :], None).then_inc(xs_out, 16)

            def release(b):
                pool.wait_ge(xs_out, (b + 1) * (16 * SCATTERS))
                pool.sem_inc(rows_free, 1)

            def query_rest(b, h):
                pool.wait_ge(act_qh, 8 * b + h + 1)
                pool.tensor_tensor(qT[1][:, h % 2, :], qT_in[:, h % 2, :], qT[0][:, h % 2, :].bitcast(F32),
                                   ALU.subtract).then_inc(pool_ql, 1)

            def split_expert(e):
                pool.wait_ge(ld_gu[e % 2], 32 * (e // 2 + 1))
                pool.tensor_copy(wgu_sb[0][:, e, :], wgu_in[:, e % 2, :]).then_inc(pool_step, 1)
                pool.wait_ge(pool_step, e + 1)
                pool.tensor_tensor(wgu_sb[1][:, e, :], wgu_in[:, e % 2, :],
                                   wgu_sb[0][:, e, :].bitcast(F32), ALU.subtract).then_inc(pool_gu, 1)

            def body(b, last):
                dispatch(b - 2, 0, SCATTERS // 2)
                query_rest(b, 1)
                dispatch(b - 2, SCATTERS // 2, SCATTERS)
                release(b - 2)
                if not last:
                    rstds(b + 1, 0)
                query_rest(b, 2)
                rstds(b - 1, 1)
                for h in range(3, H):
                    query_rest(b, h)
                if not last:
                    query_rest(b + 1, 0)

            pool.sem_inc(rows_free, 1)
            pool.wait_ge(ld_w, LD_W)
            rstds(0, 0)
            query_rest(0, 0)
            query_rest(0, 1)
            split_expert(0)
            split_expert(1)
            rstds(1, 0)
            for h in range(2, H):
                query_rest(0, h)
                split_expert(h)
            query_rest(1, 0)
            query_rest(1, 1)
            rstds(2, 0)
            query_rest(1, 2)
            rstds(0, 1)
            split_expert(E - 1)
            for h in range(3, H):
                query_rest(1, h)
            query_rest(2, 0)
            with pool.Fori(2, B - 1) as b:
                body(b, False)
            body(B - 1, True)
            dispatch(B - 2, 0, SCATTERS)
            release(B - 2)
            rstds(B - 1, 1)
            dispatch(B - 1, 0, SCATTERS)
            with pool.Fori(0, GROUPS) as g:
                for i in range(NX):
                    pool.wait_ge(m_ys, g * NX + i + 1)
                    passed(pool)
                    pool.indirect_dma_start(
                        y_dram[:, :], bass.IndirectOffsetOnAxis(ap=xs[:, i, D:D + 1].bitcast(I32), axis=0),
                        ys[:, i, :], None).then_inc(y_out[i], 16)

        @block.tensor
        def _(pe):
            def pairs(out, w, x, start=True, stop=True):
                pe.matmul(out, w[0], x[0], start=start, stop=False)
                pe.matmul(out, w[0], x[1], start=False, stop=False)
                return pe.matmul(out, w[1], x[0], start=False, stop=stop)

            def cols(pair, a, b):
                return [t[:, a:b] for t in pair]

            def project_x(b, first):
                pe.wait_ge(dve_xn, b + 1)
                if not first:
                    pe.wait_ge(dve_lg, b - 1)
                for t in range(QT):
                    last = pe.transpose(b_bank[:, t * 128:(t + 1) * 128], xn[:, t, :], ident)
                last.then_inc(pe_xnT, 1)

            def project_kv(b):
                pe.wait_ge(dve_xl, b + 1)
                if not isinstance(b, int) or b > 0:
                    pe.wait_ge(dve_q, 8 * b)
                pairs(a_bank[:, :], cols(wkv_sb, 0, D), cols(xnT, 0, T)).then_inc(pe_k, 1)
                pairs(b_bank[:, :], cols(wkv_sb, D, 2 * D), cols(xnT, 0, T)).then_inc(pe_v, 1)

            def values(b, kt):
                if kt == 0:
                    pe.wait_ge(dve_vl, b + 1)
                for i in range(2):
                    if kt > 1:
                        pe.wait_ge((act_vw, dve_vw)[i], 4 * b + kt - 1)
                    elif i == 1 and kt == 0:
                        pe.wait_ge(dve_q, 8 * b + 3)
                    out_bank = (t_bank, (a_bank, b_bank))[i][kt % 2]
                    pairs(out_bank[:, :], cols(vT, kt * 128, (kt + 1) * 128),
                          cols(wo_sb, i * 512, (i + 1) * 512)).then_inc(pe_vw, 1)

            def queries(b, h):
                if h == 0:
                    pe.wait_ge(dve_kT, b + 1)
                elif h == 3:
                    pe.wait_ge(dve_vw, 4 * b + 3)
                else:
                    pe.wait_ge(dve_q, 8 * b + h)
                pairs(a_bank[:, :], cols(wq_sb, h * D, (h + 1) * D), cols(xnT, 0, T)).then_inc(pe_q, 1)

            def scores(b, h, qt, odd):
                w = (qt + 1) * 128
                if qt == 0:
                    pe.wait_ge(dve_q, 8 * b + h + 1)
                    ins = pe.matmul(s_bank[0], qT_in[:, h % 2, 0:128], kT_in[:, odd, 0:w], start=True, stop=True)
                else:
                    if qt == 1:
                        pe.wait_ge(pool_ql, 8 * b + h + 1)
                        if h == 0:
                            pe.wait_ge(dve_kl, b + 1)
                    ins = pairs(s_bank[qt], [q[:, h % 2, qt * 128:w] for q in qT],
                                [k[:, odd, 0:w] for k in kT])
                ins.then_inc(pe_s, 1)

            def transposes(b, h, qt):
                n = 32 * b + 4 * h + qt
                if h == 0 and qt < 2:
                    pe.wait_ge(act_vw, 4 * b + 3 + qt)
                else:
                    pe.wait_ge(act_pT, n - 1)
                pe.wait_ge(dve_pn, n + 1)
                for kt in range(qt + 1):
                    last = pe.transpose(t_bank[qt % 2][:, kt * 128:(kt + 1) * 128],
                                        pr[:, h % 2, PR[qt] + kt * 128:PR[qt] + (kt + 1) * 128], ident)
                last.then_inc(pe_t, 1)

            def attend(b, h, first):
                pe.wait_ge(act_pT, 32 * b + 4 * h + 3)
                if h == 0:
                    pe.wait_ge(dve_vw, 4 * b + 4)
                    if not first:
                        pe.wait_ge(act_oT, b)
                q3 = (QT - 1) * 128
                for kt in range(QT - 1):
                    pe.matmul(o_bank[:, kt * 128:q3], vw[:, kt, h * D:(h + 1) * D],
                              pT[:, h % 2, kt, kt * 128:q3], start=(h == 0 and kt == 0),
                              stop=False)
                pe.wait_ge(act_pT, 32 * b + 4 * h + 4)
                for kt in range(QT):
                    last = pe.matmul(o_bank[:, q3:], vw[:, kt, h * D:(h + 1) * D],
                                     pT[:, h % 2, kt, q3:], start=False,
                                     stop=(h == H - 1 and kt == QT - 1))
                last.then_inc(pe_av, 1)

            def residual(b, in_body):
                pe.wait_ge(act_oT, b + 1)
                if in_body:
                    pe.wait_ge(dve_vw, 4 * b + 8)
                else:
                    pe.wait_ge(dve_slot, b)
                for t in range(QT):
                    last = pe.transpose(b_bank[:, t * 128:(t + 1) * 128], oT[:, t * 128:(t + 1) * 128], ident)
                last.then_inc(pe_x2, 1)

            def normed(b):
                pe.wait_ge(dve_x2n, b + 1)
                for t in range(QT):
                    last = pe.transpose(b_bank[:, t * 128:(t + 1) * 128], payload[:, t, 0, 0:D], ident)
                last.then_inc(pe_xn2T, 1)

            def logits(b):
                pe.wait_ge(act_xn2T, b + 1)
                for t in range(QT):
                    last = pe.matmul(b_bank[:, t * E:(t + 1) * E], xn2T[:, t * 128:(t + 1) * 128], wr_sb[:, :],
                                     start=True, stop=True)
                last.then_inc(pe_lg, 1)

            def ranks(b, in_body):
                if in_body:
                    pe.wait_ge(dve_vl, b + 3)
                pe.wait_ge(dve_oh, b + 1)
                w = QT * E
                pe.matmul(b_bank[:, 64:64 + w], lt_bf[:, :], oh_bf[:, :], start=True, stop=False)
                for t in range(1, QT):
                    pe.matmul(b_bank[:, 64 + t * E:64 + w], one_bf[:, :], oh_bf[:, 0:w - t * E],
                              start=False, stop=(t == QT - 1))
                for t in range(QT):
                    last = pe.matmul(b_bank[:, 128:128 + E], one_bf[:, :], oh_bf[:, t * E:(t + 1) * E],
                                     start=(t == 0), stop=(t == QT - 1))
                last.then_inc(pe_cnt, 1)

            def body(b, first, last, odd):
                for s in range(H):
                    prev = (b, s - 1) if s else (b - 1, H - 1)
                    behind = s > 0 or not first
                    if 0 < s < H - 2:
                        queries(b, s + 2)
                    if behind:
                        transposes(*prev, 0)
                        transposes(*prev, 1)
                    scores(b, s, 0, odd)
                    scores(b, s, 1, odd)
                    if behind:
                        transposes(*prev, 2)
                    scores(b, s, 2, odd)
                    if behind:
                        transposes(*prev, 3)
                    scores(b, s, 3, odd)
                    if not first and s == 4:
                        logits(b - 1)
                    if not first and s == (H - 2 if last else H - 1):
                        ranks(b - 1, not last)
                    if not last:
                        if s == H - 3:
                            project_x(b + 1, first)
                        if s == H - 2:
                            project_kv(b + 1)
                    if behind:
                        attend(*prev, first or s == 0)
                    if s == 0:
                        queries(b, 2)
                        for kt in range(QT):
                            values(b, kt)
                    if not first and s == 1:
                        residual(b - 1, True)
                    if not first and s == 3:
                        normed(b - 1)
                    if s >= H - 2 and not last:
                        queries(b + 1, s - (H - 2))

            pe.wait_ge(ld_w, LD_W)
            project_x(0, True)
            pe.wait_ge(dve_wlo, 3)
            project_kv(0)
            queries(0, 0)
            queries(0, 1)
            body(0, True, False, 0)
            with pe.Fori(1, B - 2, 2) as b:
                body(b, False, False, 1)
                body(b + 1, False, False, 0)
            body(B - 1, False, True, 1)
            for qt in range(QT):
                transposes(B - 1, H - 1, qt)
            attend(B - 1, H - 1, False)
            residual(B - 1, False)
            normed(B - 1)
            logits(B - 1)
            ranks(B - 1, False)

            def flat(w):
                return w[:, :, :].rearrange("p e n -> p (e n)")
            wgu_flat = [flat(w) for w in wgu_sb]
            wd_flat = wd_sb[:, :, :, :].rearrange("p e c n -> p (e c n)")

            def experts(j, n):
                return nc.values_load_multi_w_load_instructions(
                    e_tab[0:1, bass.ds(j, n)], engines=(mybir.EngineType.PE,), min_val=0, max_val=E - 1,
                    skip_runtime_bounds_check_because="VectorE clamps them to the experts")[1]

            def m_transpose(g, i):
                pe.wait_ge(xs_in[i], g * 16 + 16)
                pe.transpose(bank[i % 2][:, 0:D], xs[:, i, 0:D], ident).then_inc(m_xT, 1)

            def m_product(g, i, e, up):
                if not up:
                    pe.wait_ge(m_xTl, g * NX + i + 1)
                at = e * (2 * I) + (I if up else 0)
                pairs(bank[(4 if up else 2) + i % 2][:, 0:I], [x[:, i % 2, :] for x in xsT],
                      [w[:, bass.ds(at, I)] for w in wgu_flat]).then_inc(m_u if up else m_g, 1)

            def m_hidden_t(g, i):
                j = g * NX + i
                pe.wait_ge(m_hid, j + 1)
                if not (isinstance(g, int) and j < 1):
                    pe.wait_ge(m_hTc, j)
                for c in range(IC):
                    last = pe.transpose(bank[6][:, c * 128:(c + 1) * 128],
                                        hid[:, i % 2, c * 128:(c + 1) * 128], ident)
                last.then_inc(m_hT, 1)

            def m_down(g, i, e, last_tile=False):
                j = g * NX + i
                if last_tile:
                    pe.wait_ge(m_hTc, j + 1)
                if not (isinstance(g, int) and j < 1):
                    pe.wait_ge(m_ys, j)
                for c in range(IC):
                    last = pe.matmul(bank[7][:, 0:D], hidT[:, i % 2, c * 128:(c + 1) * 128],
                                     wd_flat[:, bass.ds(e * (IC * D) + c * D, D)], start=(c == 0),
                                     stop=(c == IC - 1))
                last.then_inc(m_y, 1)

            def tile(g, i):
                return (g + i // NX, i % NX)

            def expert_group(g, first, last):
                for i in range(NX):
                    if i == 0 and not first:
                        old = experts(g * NX - 2, 2)
                    if i % 4 == 0:
                        e = (list(e) if i else []) + list(experts(g * NX + i, 4))
                    if not (last and i == NX - 1):
                        m_transpose(*tile(g, i + 1))
                    m_product(g, i, e[i], False)
                    if not (first and i == 0):
                        m_hidden_t(*tile(g, i - 1))
                    m_product(g, i, e[i], True)
                    if not (first and i < 2):
                        m_down(*tile(g, i - 2), old[i] if i < 2 else e[i - 2])

            pe.wait_ge(dve_tab, 2)
            pe.wait_ge(ld_moe, LD_MOE)
            pe.wait_ge(pool_gu, E)
            m_transpose(0, 0)
            expert_group(0, True, False)
            with pe.Fori(1, GROUPS - 1) as g:
                expert_group(g, False, False)
            expert_group(GROUPS - 1, False, True)
            old = experts(TILES - 2, 2)
            m_hidden_t(GROUPS - 1, NX - 1)
            m_down(GROUPS - 1, NX - 2, old[0])
            m_down(GROUPS - 1, NX - 1, old[1], last_tile=True)

        @block.scalar
        def _(act):
            def project_x(b):
                act.wait_ge(pe_xnT, b + 1)
                act.copy(xnT[0][:, :], b_bank[:, :]).then_inc(act_xnT, 1)

            def project_kv(b, odd):
                act.wait_ge(dve_kT, b + 1)
                act.copy(kT[0][:, odd, :], kT_in[:, odd, :]).then_inc(act_kh, 1)
                act.wait_ge(pe_v, b + 1)
                act.activation(vT[0][:, :], b_bank[:, :], ACT.Identity, bias=bkv_sb[:, 1:2]).then_inc(act_vT, 1)

            def values(b, kt):
                act.wait_ge(pe_vw, 8 * b + 2 * kt + 1)
                act.copy(vw[:, kt, 0:512], t_bank[kt % 2][:, :]).then_inc(act_vw, 1)

            def output(b):
                act.wait_ge(pe_av, 8 * b + 8)
                act.copy(oT[:, :], o_bank[:, :]).then_inc(act_oT, 1)

            def queries(b, h):
                act.wait_ge(dve_q, 8 * b + h + 1)
                act.copy(qT[0][:, h % 2, :], qT_in[:, h % 2, :]).then_inc(act_qh, 1)

            def exps(b, h, qt):
                act.wait_ge(dve_negs, 32 * b + 4 * h + qt + 1)
                p = pr[:, h % 2, PR[qt]:PR[qt + 1]]
                act.activation(p, p, ACT.Exp,
                               bias=nmax[:, h % 2, qt:qt + 1], scale=-1.0,
                               accum_out=rsum[:, h % 2, qt:qt + 1]).then_inc(act_p, 1)

            def evacuate(b, h, qt, first):
                act.wait_ge(pe_t, 32 * b + 4 * h + qt + 1)
                if qt == 0 and not (first and h < 2):
                    act.wait_ge(pe_av, 8 * b + h - 1)
                act.copy(pT[:, h % 2, 0:qt + 1, qt * 128:(qt + 1) * 128],
                         t_bank[qt % 2][:, 0:(qt + 1) * 128].rearrange("p (k q) -> p k q", q=128)).then_inc(act_pT, 1)

            def body(b, first, last, odd):
                for s in range(H):
                    prev = (b, s - 1) if s else (b - 1, H - 1)
                    behind = s > 0 or not first
                    if behind:
                        evacuate(*prev, 0, first)
                        evacuate(*prev, 1, first)
                    if 0 < s < H - 1:
                        queries(b, s + 1)
                    if s == 4 and not first:
                        act.wait_ge(pe_xn2T, b)
                        act.copy(xn2T[:, :], b_bank[:, :]).then_inc(act_xn2T, 1)
                    if behind:
                        evacuate(*prev, 2, first)
                    exps(b, s, 0)
                    exps(b, s, 1)
                    if behind:
                        evacuate(*prev, 3, first)
                    exps(b, s, 2)
                    exps(b, s, 3)
                    if s == 0:
                        queries(b, 1)
                    elif s == H - 1 and not last:
                        queries(b + 1, 0)
                    if s == 6 and not first:
                        act.wait_ge(dve_gap, b)
                        act.activation(e2[:, :], gap[:, :], ACT.Exp).then_inc(act_e2, 1)
                    if not last:
                        if s == H - 3:
                            project_x(b + 1)
                        if s == H - 2:
                            project_kv(b + 1, 1 - odd)
                    if s == 0:
                        if not first:
                            output(b - 1)
                        for kt in range(QT):
                            values(b, kt)

            act.wait_ge(ld_w, LD_W)
            for w, w_in in ((wkv_sb, wkv_in), (wq_sb, wq_in), (wo_sb, wo_in)):
                act.copy(w[0][:, :], w_in).then_inc(act_whi, 1)
            project_x(0)
            project_kv(0, 0)
            queries(0, 0)
            body(0, True, False, 0)
            with act.Fori(1, B - 2, 2) as b:
                body(b, False, False, 1)
                body(b + 1, False, False, 0)
            body(B - 1, False, True, 1)
            for qt in range(QT):
                evacuate(B - 1, H - 1, qt, False)
            output(B - 1)
            act.wait_ge(pe_xn2T, B)
            act.copy(xn2T[:, :], b_bank[:, :]).then_inc(act_xn2T, 1)
            act.wait_ge(dve_gap, B)
            act.activation(e2[:, :], gap[:, :], ACT.Exp).then_inc(act_e2, 1)
            act.preload_act_table(ACT.Silu)

            def m_rows(g, i):
                j = g * NX + i
                act.wait_ge(m_xT, j + 1)
                act.copy(xsT[0][:, i % 2, :], bank[i % 2][:, 0:D]).then_inc(m_xTc, 1)

            def m_silu(g, i):
                j = g * NX + i
                act.wait_ge(m_g, j + 1)
                act.activation(sg[:, i % 2, :], bank[2 + i % 2][:, 0:I], ACT.Silu).then_inc(m_sg, 1)

            def m_result(g, i):
                j = g * NX + i
                act.wait_ge(m_y, j + 1)
                act.activation(ys[:, i, :], bank[7][:, 0:D], ACT.Copy,
                               scale=xs[:, i, D + 1:D + 2]).then_inc(m_ys, 1)

            def tile(g, i):
                return (g + i // NX, i % NX)

            def expert_group(g, first, last):
                for i in range(NX):
                    if not (last and i == NX - 1):
                        m_rows(*tile(g, i + 1))
                    m_silu(g, i)
                    if not (first and i < 2):
                        m_result(*tile(g, i - 2))

            m_rows(0, 0)
            expert_group(0, True, False)
            with act.Fori(1, GROUPS - 1) as g:
                expert_group(g, False, False)
            expert_group(GROUPS - 1, False, True)
            m_result(GROUPS - 1, NX - 2)
            m_result(GROUPS - 1, NX - 1)

        @block.vector
        def _(dve):
            count = {"base": 0, "n": 0}

            def link(ins):
                count["n"] += 1
                ins.then_inc(dve_step, 1)
                dve.wait_ge(dve_step, count["base"] + count["n"])

            def x_tile(b, t):
                return x_all[:, bass.ds(b * T + t * D, D)]

            def moments(b, which, st_, mv_):
                if not isinstance(b, int):
                    passed(dve)
                for t in range(QT):
                    ins = dve.bn_stats(st_[:, t, :], x_tile(b, t))
                link(ins)
                if not isinstance(b, int):
                    passed(dve)
                for t in range(QT):
                    ins = dve.bn_aggr(mv_[:, t, :], st_[:, t, :])
                link(ins)
                dve.tensor_scalar(veps[:, which, :], mv_[:, :, 1], EPS, None, ALU.add).then_inc(dve_var[which], 1)

            def norm_in(b):
                if not isinstance(b, int) or b > 0:
                    dve.wait_ge(pe_xnT, b)
                dve.wait_ge(pool_rstd[0], b + 1)
                for t in range(QT):
                    ins = dve.tensor_scalar(xn[:, t, :], x_tile(b, t), mv[:, t, 0:1], rstd[:, 0, t:t + 1],
                                            ALU.subtract, ALU.mult)
                ins.then_inc(dve_xn, 1)

            def x_rest(b):
                dve.wait_ge(act_xnT, b + 1)
                dve.tensor_tensor(xnT[1][:, :], b_bank[:, :], xnT[0][:, :].bitcast(F32),
                                  ALU.subtract).then_inc(dve_xl, 1)

            def keys(b, odd):
                dve.wait_ge(pe_k, b + 1)
                dve.scalar_tensor_tensor(out=kT_in[:, odd, :], in0=a_bank[:, :], scalar=bkv_sb[:, 0:1],
                                         in1=pe_sb[:, :], op0=ALU.add, op1=ALU.add).then_inc(dve_kT, 1)

            def key_value_rests(b, odd):
                dve.wait_ge(act_kh, b + 1)
                dve.tensor_tensor(kT[1][:, odd, :], kT_in[:, odd, :], kT[0][:, odd, :].bitcast(F32),
                                  ALU.subtract).then_inc(dve_kl, 1)
                dve.wait_ge(act_vT, b + 1)
                dve.scalar_tensor_tensor(out=vT[1][:, :], in0=b_bank[:, :], scalar=bkv_sb[:, 1:2],
                                         in1=vT[0][:, :].bitcast(F32), op0=ALU.add,
                                         op1=ALU.subtract).then_inc(dve_vl, 1)

            def values(b, kt):
                dve.wait_ge(pe_vw, 8 * b + 2 * kt + 2)
                dve.tensor_copy(vw[:, kt, 512:1024], (a_bank, b_bank)[kt % 2][:, :]).then_inc(dve_vw, 1)

            def queries(b, h):
                dve.wait_ge(pe_q, 8 * b + h + 1)
                dve.scalar_tensor_tensor(out=qT_in[:, h % 2, :], in0=a_bank[:, :], scalar=bq_sb[:, h:h + 1],
                                         in1=pe_sb[:, :], op0=ALU.add, op1=ALU.add).then_inc(dve_q, 1)

            def masked(b, h, qt):
                n = 32 * b + 4 * h + qt
                dve.wait_ge(pe_s, n + (2 if qt == 0 else 1))
                w = (qt + 1) * 128
                if not isinstance(b, int):
                    passed(dve)
                dve.tensor_tensor_reduce(out=pr[:, h % 2, PR[qt]:PR[qt + 1]], in0=s_bank[qt],
                                         in1=cst[:, C_MASK + T - w:C_MASK + T], scale=-SCALE, scalar=BIG,
                                         op0=ALU.add, op1=ALU.min,
                                         accum_out=nmax[:, h % 2, qt:qt + 1]).then_inc(dve_negs, 1)

            def normalise(b, h):
                def inverse(q0, q1):
                    dve.wait_ge(act_p, 32 * b + 4 * h + q1)
                    count["n"] += 1
                    dve.reciprocal(rinv[:, h % 2, q0:q1], rsum[:, h % 2, q0:q1]).then_inc(dve_step, 1)

                def scale(qt):
                    p = pr[:, h % 2, PR[qt]:PR[qt + 1]]
                    dve.tensor_scalar(p, p, rinv[:, h % 2, qt:qt + 1], None, ALU.mult).then_inc(dve_pn, 1)
                inverse(0, 3)
                dve.wait_ge(dve_step, count["base"] + count["n"])
                scale(0)
                scale(1)
                inverse(3, 4)
                scale(2)
                dve.wait_ge(dve_step, count["base"] + count["n"])
                scale(3)

            def residual(b):
                dve.wait_ge(pe_x2, b + 1)
                xb = x_all[:, bass.ds(b * T, T)]
                link(dve.tensor_tensor(xb, b_bank[:, :], xb, ALU.add))
                moments(b, 1, stats2, mv2)

            def norm_mid(b):
                dve.wait_ge(rows_free, b + 1)
                dve.wait_ge(pool_rstd[1], b + 1)
                for t in range(QT):
                    dve.tensor_scalar(payload[:, t, :, 0:D],
                                      x_tile(b, t).rearrange("p (o d) -> p o d", o=1).broadcast_to((128, TOPK, D)),
                                      mv2[:, t, 0:1], rstd[:, 1, t:t + 1], ALU.subtract, ALU.mult)
                d = payload[:, :, :, D].bitcast(I32)
                dve.tensor_scalar(d, d, T, None, ALU.add).then_inc(dve_x2n, 1)

            def e3(ap):
                return ap.rearrange("p (t e) -> p t e", e=E)

            def b3(ap):
                return ap.rearrange("p (t o) -> p t o", o=1).broadcast_to((128, QT, E))

            def choose(b, k):
                if k == 0:
                    dve.wait_ge(pe_lg, b + 1)
                    dve.tensor_copy(lg[:, 0, :], b_bank[:, 0:QT * E]).then_inc(dve_lg, 1)
                    dve.wait_ge(dve_lg, b + 1)
                link(dve.reduce_max(top[:, k, :], e3(lg[:, k, :]), AX.X))
                link(dve.tensor_tensor(e3(iseq[:, :]), e3(lg[:, k, :]), b3(top[:, k, :]), ALU.is_ge))
                link(dve.tensor_tensor(key[:, :], iseq[:, :], cst[:, C_REV:C_REV + QT * E], ALU.mult))
                link(dve.reduce_max(kmax[:, :], e3(key[:, :]), AX.X))
                link(dve.tensor_tensor(e3(oh[:, k, :]), e3(key[:, :]), b3(kmax[:, :]), ALU.is_equal))
                if k == 0:
                    link(dve.scalar_tensor_tensor(out=lg[:, 1, :], in0=oh[:, 0, :], scalar=-BIG,
                                                  in1=lg[:, 0, :], op0=ALU.mult, op1=ALU.add))
                else:
                    dve.tensor_tensor(oh_bf[:, :], oh[:, 0, :], oh[:, 1, :], ALU.add).then_inc(dve_oh, 1)
                    dve.tensor_tensor(gap[:, :], top[:, 1, :], top[:, 0, :], ALU.subtract).then_inc(dve_gap, 1)

            def place(b):
                dve.wait_ge(act_e2, b + 1)
                link(dve.tensor_scalar(den[:, :], e2[:, :], 1.0, None, ALU.add))
                link(dve.reciprocal(wrow[:, :, 0], den[:, :]))
                link(dve.tensor_tensor(wrow[:, :, 1], e2[:, :], wrow[:, :, 0], ALU.mult))
                dve.tensor_copy(payload[:, :, :, D + 1], wrow[:, :, :])
                dve.wait_ge(pe_cnt, b + 1)
                link(dve.tensor_tensor(
                    e3(pos[:, :]), e3(b_bank[:, 64:64 + QT * E]),
                    fill[:, :].rearrange("p (o e) -> p o e", o=1).broadcast_to((128, QT, E)), ALU.add))
                for k in range(TOPK):
                    link(dve.tensor_tensor(posk[:, k, :], oh[:, k, :], pos[:, :], ALU.mult))
                    link(dve.reduce_sum(slot_f[:, k, :], e3(posk[:, k, :]), AX.X))
                link(dve.tensor_tensor(fill[:, :], fill[:, :], b_bank[:, 128:128 + E], ALU.add))
                dve.tensor_copy(slot[:, :, :], slot_f[:, :, :]).then_inc(dve_slot, 1)

            def body(b, first, last, odd):
                at = count["n"]
                for s in range(H):
                    for qt in range(QT):
                        masked(b, s, qt)
                    if s == 0:
                        queries(b, 1)
                    elif s + 2 < H:
                        queries(b, s + 2)
                    elif s == H - 1 and not last:
                        queries(b + 1, 0)
                    normalise(b, s)
                    if s == 0:
                        queries(b, 2)
                    if s == 0:
                        for kt in range(QT):
                            values(b, kt)
                    if not last:
                        if s == 0:
                            moments(b + 1, 0, stats, mv)
                        if s == 3:
                            norm_in(b + 1)
                        if s == H - 3:
                            x_rest(b + 1)
                        if s == H - 2:
                            keys(b + 1, 1 - odd)
                            key_value_rests(b + 1, 1 - odd)
                    if not first:
                        if s == 1:
                            residual(b - 1)
                        if s == 2:
                            norm_mid(b - 1)
                        if s == 4:
                            choose(b - 1, 0)
                        if s == 5:
                            choose(b - 1, 1)
                        if s == (H - 2 if last else H - 1):
                            place(b - 1)
                assert first or last or count["n"] - at == STEPS

            dve.wait_ge(ld_x0, 16)
            moments(0, 0, stats, mv)
            norm_in(0)
            dve.wait_ge(ld_w, LD_W)
            for n, (w, w_in) in enumerate(((wkv_sb, wkv_in), (wq_sb, wq_in), (wo_sb, wo_in))):
                dve.wait_ge(act_whi, n + 1)
                dve.tensor_tensor(w[1][:, :], w_in, w[0][:, :].bitcast(F32), ALU.subtract).then_inc(dve_wlo, 1)
            x_rest(0)
            dve.memset(wd_sb[96:128, :, IC - 1, :], 0.0).then_inc(wd_zero, 1)
            link(dve.memset(padrows[:, :, :], 0.0))
            keys(0, 0)
            key_value_rests(0, 0)
            queries(0, 0)
            dve.tensor_copy(lt_bf[:, :], cst[:, C_LT:C_LT + 128])
            dve.tensor_copy(one_bf[:, :], cst[:, C_ONE:C_ONE + 128]).then_inc(cast_done, 1)
            dve.tensor_copy(fill[:, :], cst[:, C_CAP:C_CAP + E])
            link(dve.tensor_copy(payload[:, :, :, D].bitcast(I32),
                                 dst0[:, 0:SCATTERS].rearrange("p (t k) -> p t k", k=TOPK)))
            dve.tensor_copy(padrows[:, :, D].bitcast(I32), dst0[:, SCATTERS:]).then_inc(pad_ready, 1)
            dve.wait_ge(ld_x, 16 * (B - 1))
            body(0, True, False, 0)
            count["base"], count["n"] = count["n"], 0
            before = count["base"]
            with dve.Fori(1, B - 2, 2) as b:
                count["base"], count["n"] = (b - 1) * STEPS + before, 0
                body(b, False, False, 1)
                body(b + 1, False, False, 0)
            count["base"], count["n"] = before + (B - 2) * STEPS, 0
            body(B - 1, False, True, 1)
            residual(B - 1)
            norm_mid(B - 1)
            choose(B - 1, 0)
            choose(B - 1, 1)
            place(B - 1)

            dve.memset(hid[:, :, I:IP], 0.0)
            dve.tensor_copy(fill_i[:, :], fill[:, :]).then_inc(dve_tab, 1)
            link(dve.tensor_tensor(cnt[:, :], fill[:, :], cst[:, C_CAP:C_CAP + E], ALU.subtract))

            def wide(ap, n):
                return ap.rearrange("p (m o) -> p m o", o=1).broadcast_to((128, ap.shape[1], n))

            def tall(ap, n):
                return ap.rearrange("p (o m) -> p o m", o=1).broadcast_to((128, n, ap.shape[1]))

            link(dve.tensor_tensor(over[:, :].rearrange("p (e m) -> p e m", m=NT), wide(cnt[:, :], NT),
                                   tall(cst[:, C_THR:C_THR + NT], E), ALU.is_gt))
            link(dve.reduce_sum(ntile[:, :], over[:, :].rearrange("p (e m) -> p e m", m=NT), AX.X))
            link(dve.tensor_tensor(cumm[:, :].rearrange("p (e f) -> p e f", f=E),
                                   cst[:, C_LE:C_LE + E * E].rearrange("p (e f) -> p e f", f=E),
                                   tall(ntile[:, :], E), ALU.mult))
            link(dve.reduce_sum(cum[:, :], cumm[:, :].rearrange("p (e f) -> p e f", f=E), AX.X))
            j3 = done[:, :].rearrange("p (j e) -> p j e", e=E)
            k3 = skip[:, :].rearrange("p (j e) -> p j e", e=E)
            link(dve.tensor_tensor(j3, tall(cum[:, :], TILES), wide(cst[:, C_J:C_J + TILES], E), ALU.is_le))
            link(dve.reduce_sum(ej[:, :], j3, AX.X))
            link(dve.tensor_tensor(k3, j3, tall(ntile[:, :], TILES), ALU.mult))
            link(dve.reduce_sum(st[:, :], k3, AX.X))
            link(dve.tensor_tensor(st[:, :], cst[:, C_J:C_J + TILES], st[:, :], ALU.subtract))
            link(dve.tensor_scalar(st[:, :], st[:, :], 128.0, None, ALU.mult))
            link(dve.scalar_tensor_tensor(out=rowf[:, :], in0=ej[:, :], scalar=float(CAP), in1=st[:, :],
                                          op0=ALU.mult, op1=ALU.add))
            dve.tensor_copy(row_tab[:, :], rowf[:, :])
            dve.tensor_scalar(e_tab[:, :], ej[:, :], float(E - 1), None, ALU.min).then_inc(dve_tab, 1)

            def m_hidden(g, i):
                j = g * NX + i
                dve.wait_ge(m_sg, j + 1)
                dve.wait_ge(m_u, j + 1)
                dve.tensor_tensor(hid[:, i % 2, 0:I], sg[:, i % 2, :], bank[4 + i % 2][:, 0:I],
                                  ALU.mult).then_inc(m_hid, 1)

            def m_hidden_t(g, i):
                j = g * NX + i
                dve.wait_ge(m_hT, j + 1)
                dve.tensor_copy(hidT[:, i % 2, :], bank[6][:, 0:IP]).then_inc(m_hTc, 1)

            def m_rows_rest(g, i):
                dve.wait_ge(m_xTc, g * NX + i + 1)
                dve.tensor_tensor(xsT[1][:, i % 2, :], bank[i % 2][:, 0:D], xsT[0][:, i % 2, :].bitcast(F32),
                                  ALU.subtract).then_inc(m_xTl, 1)

            def tile(g, i):
                return (g + i // NX, i % NX)

            def expert_group(g, first, last):
                for i in range(NX):
                    if not (last and i == NX - 1):
                        m_rows_rest(*tile(g, i + 1))
                    if not (first and i == 0):
                        m_hidden_t(*tile(g, i - 1))
                    m_hidden(g, i)

            m_rows_rest(0, 0)
            expert_group(0, True, False)
            with dve.Fori(1, GROUPS - 1) as g:
                expert_group(g, False, False)
            expert_group(GROUPS - 1, False, True)
            m_hidden_t(GROUPS - 1, NX - 1)

            for b in range(B):
                dve.wait_ge(y_ld[b], 16 * TOPK)
                xb = x_all[:, b * T:(b + 1) * T]
                link(dve.tensor_tensor(xb, xb, y_in[b][0], ALU.add))
                dve.tensor_tensor(xb, xb, y_in[b][1], ALU.add).then_inc(dve_fin, 1)


INPUTS = ("L0_attn_x", "L0_attn_Wq", "L0_attn_bq", "L0_attn_Wkv", "L0_attn_bkv", "L0_attn_Wo",
          "L0_ffn_Wr", "L0_ffn_Wg", "L0_ffn_Wu", "L0_ffn_Wd")


def kernel(**inputs):
    import concourse.bacc as bacc
    from concourse.bass_utils import run_bass_kernel_spmd

    nc = bacc.Bacc("TRN2", target_bir_lowering=False, num_devices=1)
    given = [(n, np.ascontiguousarray(inputs[n])) for n in INPUTS]
    given += list(zip(("consts", "dest", "positions"), constants()))
    given = [(n, np.ascontiguousarray(a.reshape(-1, D).T) if n in ("L0_attn_bq", "L0_attn_bkv") else a)
             for n, a in given]
    arrays, args = {}, []
    for name, a in given:
        arrays[name] = a
        args.append(nc.dram_tensor(name, a.shape, mybir.dt.from_np(a.dtype), kind="ExternalInput").ap())
    out = nc.dram_tensor("out", (B, T, D), F32, kind="ExternalOutput").ap()
    block_kernel(nc, *args, out)
    r = run_bass_kernel_spmd(nc, [arrays], core_ids=[0])
    return r.results[0]["out"]
```

```python
from contextlib import ExitStack

import numpy as np

import concourse.bass as bass
from concourse import mybir

F32, F32R = mybir.dt.float32, mybir.dt.float32r
BF16, I32 = mybir.dt.bfloat16, mybir.dt.int32
ALU = mybir.AluOpType
ACT = mybir.ActivationFunctionType
AX = mybir.AxisListType

B, T, D = 8, 512, 128
H = 8
QT = T // 128
NTOK = B * T
NT = NTOK // 128
E, I, TOPK = 9, 352, 2
IC = 3
IP = IC * 128
SCALE = float(D) ** -0.5
EPS = 1e-5
NEG = -1.0e30
BIG = 3.0e38

ROW = D + 2
CAP = NTOK + 128
NX = 8
TILES = -(-(TOPK * NTOK // 128 + E - 1) // NX) * NX
SPARE = TILES - TOPK * NTOK // 128
PADS = E + SPARE
XS_ROWS = E * CAP + SPARE * 128
Y_ROWS = TOPK * NTOK + PADS * 128
SCATTERS = QT * TOPK
GROUPS = TILES // NX
FULL = -(-(TOPK * (B - 2) * T - E * 127) // 128)
EARLY = 3 * NX
assert EARLY <= FULL
PR = [128 * (qt * (qt + 1) // 2) for qt in range(QT + 1)]

VW_ORDER = [(0, 0), (1, 0), (0, 1), (1, 1), (2, 0), (2, 1), (3, 1), (3, 0)]

STEPS = 2 * H + 2 * 2 + 1 + (5 * TOPK + 1) + 4

C_ID = 0
C_MASK = C_ID + 128
C_LT = C_MASK + T
C_REV = C_LT + 128
C_THR = C_REV + QT * E
C_LE = C_THR + NT
C_J = C_LE + E * E
C_CAP = C_J + TILES
C_END = C_CAP + E


def constants():
    c = np.zeros((128, C_END), np.float32)
    p = np.arange(128)
    c[:, C_ID:C_ID + 128] = np.eye(128)
    c[:, C_MASK + T - 128:C_MASK + T] = np.where(p[None, :] > p[:, None], NEG, 0.0)
    c[:, C_LT:C_LT + 128] = p[:, None] < p[None, :]
    c[:, C_REV:C_REV + QT * E] = np.tile(E - np.arange(E), QT)
    c[:, C_THR:C_THR + NT] = 128 * np.arange(NT)
    c[:, C_LE:C_LE + E * E] = (np.arange(E)[None, :] <= np.arange(E)[:, None]).reshape(-1)
    c[:, C_J:C_J + TILES] = np.arange(TILES)
    c[:, C_CAP:C_CAP + E] = CAP * np.arange(E)
    t, k = np.arange(QT)[:, None], np.arange(TOPK)[None, :]
    pairs = (k * NTOK + t * 128 - T).reshape(1, -1) + p[:, None]
    pads = TOPK * NTOK + 128 * np.arange(PADS)[None, :] + p[:, None]
    dest = np.concatenate([pairs, pads], 1).astype(np.int32)
    pos = np.arange(T, dtype=np.float32)[:, None]
    inv = np.exp(np.float32(-np.log(10000.0)) * np.arange(0, D, 2, dtype=np.float32) / np.float32(D))
    ang = pos * inv[None, :].astype(np.float32)
    pe = np.zeros((T, D), np.float32)
    pe[:, 0::2] = np.sin(ang)
    pe[:, 1::2] = np.cos(ang)
    return c, dest, np.ascontiguousarray(pe.T)


def block_kernel(nc, x, wq, bq, wkv, bkv, wo, wr, wg, wu, wd, consts, dest, positions, out):
    ctx = ExitStack()
    with ctx:
        def sb(name, shape, dt=F32):
            return ctx.enter_context(nc.sbuf_tensor(name, shape, dt))

        def sem(name):
            return ctx.enter_context(nc.semaphore(name))

        xs_dram = nc.dram_tensor("xs_dram", (XS_ROWS, ROW), F32, kind="Internal").ap()
        y_dram = nc.dram_tensor("y_dram", (Y_ROWS, D), F32, kind="Internal").ap()

        cst = sb("cst", [128, C_END])
        dst0 = sb("dst0", [128, SCATTERS + PADS], I32)
        pe_sb = sb("pe_sb", [128, T])
        wq_sb = [sb(f"wq_sb{i}", [128, H * D], F32R) for i in range(2)]
        wk_sb = [sb(f"wk_sb{i}", [128, D], F32R) for i in range(2)]
        wvo_sb = [sb(f"wvo_sb{i}", [128, H * D], F32R) for i in range(2)]
        bvo = sb("bvo", [128, 1])
        wr_sb = sb("wr_sb", [128, E])
        bq_sb = sb("bq_sb", [128, H])
        bkv_sb = sb("bkv_sb", [128, 2])
        wgu_sb = [sb(f"wgu_sb{i}", [128, E, 2 * I], F32R) for i in range(2)]
        wgu_in = sb("wgu_in", [128, 2, 2 * I])
        wd_sb = sb("wd_sb", [128, E, IC, D])
        lt_bf = sb("lt_bf", [128, 128], BF16)
        one_bf = sb("one_bf", [128, 128], BF16)
        ident = cst[:, C_ID:C_ID + 128]

        x_all = sb("x_all", [128, NT * D])
        stats = sb("stats", [128, QT, 6])
        mv = sb("mv", [128, QT, 2])
        veps = sb("veps", [128, 2, QT])
        rstd = sb("rstd", [128, 2, QT])
        half = sb("half", [128, QT])
        euler = sb("euler", [128, QT])
        xn = sb("xn", [128, QT, D])
        xnT = [sb(f"xnT{i}", [128, T], F32R) for i in range(2)]
        kT_in = sb("kT_in", [128, 2, T])
        kT = [sb(f"kT{i}", [128, 2, T], F32R) for i in range(2)]
        vw = sb("vw", [128, QT, H * D])
        qT_in = sb("qT_in", [128, 2, T])
        qT = [sb(f"qT{i}", [128, 2, T], F32R) for i in range(2)]
        nmax = sb("nmax", [128, 2, QT])
        rsum = sb("rsum", [128, 2, QT])
        rinv = sb("rinv", [128, 2, QT])
        pr = sb("pr", [128, 2, PR[QT]])
        pT = sb("pT", [128, 2, QT, T])
        oT = sb("oT", [128, T])

        payload = sb("payload", [128, QT, TOPK, ROW])
        stats2 = sb("stats2", [128, QT, 6])
        mv2 = sb("mv2", [128, QT, 2])
        xn2T = oT
        lg = sb("lg", [128, TOPK, QT * E])
        top = sb("top", [128, TOPK, QT])
        iseq = sb("iseq", [128, QT * E])
        key = sb("key", [128, QT * E])
        kmax = sb("kmax", [128, QT])
        oh = sb("oh", [128, TOPK, QT * E])
        oh_bf = sb("oh_bf", [128, QT * E], BF16)
        gap = sb("gap", [128, QT])
        e2 = sb("e2", [128, QT])
        den = sb("den", [128, QT])
        wrow = sb("wrow", [128, QT, TOPK])
        pos = sb("pos", [128, QT * E])
        posk = sb("posk", [128, TOPK, QT * E])
        slot_f = sb("slot_f", [128, TOPK, QT])
        slot = sb("slot", [128, TOPK, QT], I32)
        fill = sb("fill", [128, E])
        padrows = sb("padrows", [128, PADS, ROW])
        cnt = sb("cnt", [128, E])
        over = sb("over", [128, E * NT])
        ntile = sb("ntile", [128, E])
        cumm = sb("cumm", [128, E * E])
        cum = sb("cum", [128, E])
        upto = sb("upto", [128, E + 1])
        taken = sb("taken", [128, E + 1])
        rise = sb("rise", [128, E])
        ej = sb("ej", [128, TILES])
        st = sb("st", [128, TILES])
        rowf = sb("rowf", [128, TILES])
        row_tab = sb("row_tab", [128, TILES], I32)
        e_tab = sb("e_tab", [128, TILES], I32)
        fill_i = sb("fill_i", [128, E], I32)

        pr_flat = pr[:, :, :].rearrange("p a n -> p (a n)")
        pT_flat = pT[:, :, :, :].rearrange("p a k n -> p (a k n)")

        def carve(flat, shapes):
            at, views = 0, []
            for a, n in shapes:
                v = flat[:, at:at + a * n]
                views.append(v.rearrange("p (a n) -> p a n", n=n) if a > 1 else v)
                at += a * n
            return views
        ys, = carve(pr_flat, [(NX, D)])
        sg, hid, hidT = carve(pT_flat, [(2, I), (2, IP), (2, IP)])
        xs, = carve(wgu_in[:, :, :].rearrange("p a n -> p (a n)"), [(NX, ROW)])
        done = xn[:, :, :].rearrange("p t n -> p (t n)")
        skip = kT_in[:, 0, :]
        xsT = [sb(f"xsT{i}", [128, 2, D], F32R) for i in range(2)]
        wq_in, wkv_in, wo_in, wvT, wo_sum = carve(
            pT_flat, [(1, H * D), (1, 2 * D), (1, H * D), (1, D), (1, H * D // 2)])
        vw_flat = vw[:, :, :].rearrange("p k n -> p (k n)")
        y_in = [[f[:, b * T:(b + 1) * T] for f in (pT_flat, vw_flat)] for b in range(B)]

        bank = [ctx.enter_context(nc.psum_tensor(f"bank{i}", [128, 512], F32)) for i in range(8)]
        s_bank = [bank[0][:, 0:128], bank[0][:, 128:384], bank[1][:, 0:384], bank[2][:, 0:512]]
        t_bank = [bank[3], bank[4]]
        o_bank = bank[5]
        a_bank, b_bank = bank[6], bank[7]
        wvo_bank = [t_bank[0], b_bank]

        def r_bank(b):
            return bank[1] if isinstance(b, int) and b == B - 1 else b_bank

        ld_x0 = sem("ld_x0"); ld_x = sem("ld_x"); ld_kv = sem("ld_kv"); ld_q = sem("ld_q")
        ld_o = sem("ld_o"); ld_moe = sem("ld_moe"); pool_pow = sem("pool_pow"); pool_e2 = sem("pool_e2")
        pe_wvT = sem("pe_wvT"); act_wvT = sem("act_wvT"); pool_wsum = sem("pool_wsum")
        pe_wvo = sem("pe_wvo"); pe_bvo = sem("pe_bvo")
        pad_ready = sem("pad_ready"); pad_out = sem("pad_out"); pad_zero = sem("pad_zero")
        dve_step = sem("dve_step")
        act_whi = sem("act_whi"); dve_wlo = sem("dve_wlo"); ld_gu = [sem("ld_gu0"), sem("ld_gu1")]
        pool_gu = sem("pool_gu"); act_qh = sem("act_qh"); pool_ql = sem("pool_ql"); act_kh = sem("act_kh")
        dve_kl = sem("dve_kl"); pool_step = sem("pool_step"); dve_xl = sem("dve_xl"); m_xTl = sem("m_xTl")
        dve_xn = sem("dve_xn"); dve_kT = sem("dve_kT"); dve_vw = sem("dve_vw"); dve_q = sem("dve_q")
        dve_negs = sem("dve_negs"); dve_pn = sem("dve_pn"); dve_x2n = sem("dve_x2n")
        dve_oh = sem("dve_oh"); dve_gap = sem("dve_gap"); dve_slot = sem("dve_slot"); dve_lg = sem("dve_lg")
        dve_tab = sem("dve_tab")
        dve_var = [sem("dve_var0"), sem("dve_var1")]; pool_rstd = [sem("pool_rstd0"), sem("pool_rstd1")]
        pe_xnT = sem("pe_xnT"); pe_k = sem("pe_k"); pe_vw = sem("pe_vw")
        pe_q = sem("pe_q"); pe_s = sem("pe_s"); pe_t = sem("pe_t"); pe_av = sem("pe_av")
        pe_x2 = sem("pe_x2"); pe_xn2T = sem("pe_xn2T"); pe_lg = sem("pe_lg"); pe_cnt = sem("pe_cnt")
        act_xnT = sem("act_xnT"); act_vw = sem("act_vw"); act_p = sem("act_p")
        act_pT = sem("act_pT"); act_oT = sem("act_oT"); act_xn2T = sem("act_xn2T"); act_e2 = sem("act_e2")
        xs_out = sem("xs_out"); rows_free = sem("rows_free"); wd_zero = sem("wd_zero")
        waits_passed = sem("waits_passed")
        fill_out = sem("fill_out")
        xs_in = [sem(f"xs_in{i}") for i in range(NX)]
        y_out = [sem(f"y_out{i}") for i in range(NX)]
        m_xT = sem("m_xT"); m_g = sem("m_g"); m_u = sem("m_u"); m_hT = sem("m_hT"); m_y = sem("m_y")
        m_xTc = sem("m_xTc"); m_sg = sem("m_sg"); m_hid = sem("m_hid"); m_hTc = sem("m_hTc"); m_ys = sem("m_ys")
        y_ld = [sem(f"y_ld{i}") for i in range(B)]
        dve_fin = sem("dve_fin"); out_st = sem("out_st")

        LD_KV, LD_Q, LD_O = 16 * 4, 16 * 2, 16 * 3
        LD_MOE = 16 * IC

        def passed(engine):
            engine.sem_inc(waits_passed, 1)

        block = ctx.enter_context(nc.Block())

        @block.sync
        def _(sp):
            xv = x.rearrange("b (t p) d -> p (b t) d", p=128)
            xs3 = x_all[:, :].rearrange("p (t d) -> p t d", d=D)
            sp.dma_start(xs3[:, 0:QT, :], xv[:, 0:QT, :]).then_inc(ld_x0, 16)
            for dst, src in ((cst[:, :], consts), (wkv_in, wkv), (bkv_sb[:, :], bkv), (pe_sb[:, :], positions)):
                sp.dma_start(dst, src).then_inc(ld_kv, 16)
            for dst, src in ((wq_in, wq), (bq_sb[:, :], bq)):
                sp.dma_start(dst, src).then_inc(ld_q, 16)
            for dst, src in ((wo_in.rearrange("p (h n) -> p h n", n=D), wo.rearrange("(h p) n -> p h n", p=D)),
                             (wr_sb[:, :], wr), (dst0[:, :], dest)):
                sp.dma_start(dst, src).then_inc(ld_o, 16)
            for b in range(1, B):
                sp.dma_start(xs3[:, b * QT:(b + 1) * QT, :], xv[:, b * QT:(b + 1) * QT, :]).then_inc(ld_x, 16)
            for e in range(E):
                if e > 1:
                    sp.wait_ge(pool_gu, e - 1)
                for k, w in enumerate((wg, wu)):
                    sp.dma_start(wgu_in[:, e % 2, k * I:(k + 1) * I], w[e, :, :]).then_inc(ld_gu[e % 2], 16)
            for c in range(IC):
                n = min(128, I - c * 128)
                if n < 128:
                    sp.wait_ge(wd_zero, 1)
                sp.dma_start(wd_sb[0:n, :, c, :],
                             wd[:, c * 128:c * 128 + n, :].rearrange("e i n -> i e n")).then_inc(ld_moe, 16)
            sp.wait_ge(pad_ready, 1)
            sp.dma_start(xs_dram[E * CAP:XS_ROWS, :].rearrange("(m p) r -> p m r", p=128),
                         padrows[:, E:PADS, :]).then_inc(pad_out, 16)
            sp.wait_ge(dve_tab, 1)

            def table_entries(table, at, n, limit):
                return nc.values_load_multi_w_load_instructions(
                    table[0:1, bass.ds(at, n)], engines=(mybir.EngineType.SP,), min_val=0, max_val=limit,
                    skip_runtime_bounds_check_because="made of counts of tokens")[1]

            def load_tile(g, i, row):
                if not (isinstance(g, int) and g == 0):
                    sp.wait_ge(y_out[i], g * 16)
                sp.dma_start(xs[:, i, :], xs_dram[bass.ds(row, 128), :]).then_inc(xs_in[i], 16)

            def load_group(g):
                rows = []
                for i in range(0, NX, 4):
                    rows += table_entries(row_tab, g * NX + i, 4, XS_ROWS - 128)
                for i in range(NX):
                    load_tile(g, i, rows[i])

            sp.wait_ge(rows_free, B - 1)
            load_group(0)
            load_group(1)
            sp.wait_ge(dve_tab, 2)
            for n in range(0, E, 3):
                ends = table_entries(fill_i, n, 3, (E - 1) * CAP + NTOK)
                for i in range(3):
                    sp.dma_start(xs_dram[bass.ds(ends[i], 128), :], padrows[:, n + i, :]).then_inc(fill_out, 16)
            load_group(2)
            sp.wait_ge(dve_tab, 3)
            sp.wait_ge(pad_out, 16)
            sp.wait_ge(fill_out, 16 * E)
            sp.wait_ge(xs_out, 16 * SCATTERS * B)
            with sp.Fori(EARLY // NX, GROUPS) as g:
                load_group(g)
            for i in range(NX):
                sp.wait_ge(y_out[i], 16 * GROUPS)
            for b in range(B):
                for k in range(TOPK):
                    lo = k * NTOK + b * T
                    sp.dma_start(y_in[b][k].rearrange("p (t d) -> p t d", d=D),
                                 y_dram[lo:lo + T, :].rearrange("(t p) d -> p t d", p=128)).then_inc(y_ld[b], 16)
            ov = out.rearrange("b (t p) d -> p (b t) d", p=128)
            for b in range(B):
                sp.wait_ge(dve_fin, b + 1)
                sp.dma_start(ov[:, b * QT:(b + 1) * QT, :], xs3[:, b * QT:(b + 1) * QT, :]).then_inc(out_st, 16)
            sp.wait_ge(out_st, 16 * B)

        @block.gpsimd
        def _(pool):
            def rstds(b, which):
                pool.wait_ge(dve_var[which], b + 1)
                pool.tensor_tensor(rstd[:, which, :], veps[:, which, :], half[:, :],
                                   ALU.pow).then_inc(pool_rstd[which], 1)

            def dispatch(b, n, m):
                if n == 0:
                    pool.wait_ge(dve_slot, b + 1)
                    if not isinstance(b, int):
                        passed(pool)
                for i in range(n, m):
                    t, k = i // TOPK, i % TOPK
                    pool.indirect_dma_start(
                        xs_dram[:, :], bass.IndirectOffsetOnAxis(ap=slot[:, k, t:t + 1], axis=0),
                        payload[:, t, k, :], None).then_inc(xs_out, 16)

            def release(b):
                pool.wait_ge(xs_out, (b + 1) * (16 * SCATTERS))
                pool.sem_inc(rows_free, 1)

            def query_rest(b, h):
                pool.wait_ge(act_qh, 8 * b + h + 1)
                pool.tensor_tensor(qT[1][:, h % 2, :], qT_in[:, h % 2, :], qT[0][:, h % 2, :].bitcast(F32),
                                   ALU.subtract).then_inc(pool_ql, 1)

            def split_expert(e):
                pool.wait_ge(ld_gu[e % 2], 32 * (e // 2 + 1))
                pool.tensor_copy(wgu_sb[0][:, e, :], wgu_in[:, e % 2, :]).then_inc(pool_step, 1)
                pool.wait_ge(pool_step, e + 1)
                pool.tensor_tensor(wgu_sb[1][:, e, :], wgu_in[:, e % 2, :],
                                   wgu_sb[0][:, e, :].bitcast(F32), ALU.subtract).then_inc(pool_gu, 1)

            def body(b, last):
                dispatch(b - 2, 0, SCATTERS // 2)
                query_rest(b, 1)
                dispatch(b - 2, SCATTERS // 2, SCATTERS)
                release(b - 2)
                if not last:
                    rstds(b + 1, 0)
                query_rest(b, 2)
                rstds(b - 1, 1)
                for h in range(3, H):
                    query_rest(b, h)
                if not last:
                    query_rest(b + 1, 0)

            pool.sem_inc(rows_free, 1)
            pool.memset(wd_sb[96:128, :, IC - 1, :], 0.0).then_inc(wd_zero, 1)
            pool.wait_ge(wd_zero, 1)
            pool.memset(half[:, :], -0.5).then_inc(pool_pow, 1)
            pool.wait_ge(pool_pow, 1)
            pool.memset(euler[:, :], float(np.e)).then_inc(pool_pow, 1)
            pool.wait_ge(pool_pow, 2)
            rstds(0, 0)
            pool.memset(padrows[:, :, :], 0.0).then_inc(pad_zero, 1)
            pool.wait_ge(pad_zero, 1)
            pool.wait_ge(ld_o, LD_O)
            n, halves = H * D // 2, wo_in
            for i in range(3):
                if i > 0:
                    pool.wait_ge(pool_wsum, i)
                pool.tensor_tensor(wo_sum[:, 0:n], halves[:, 0:n], halves[:, n:2 * n],
                                   ALU.add).then_inc(pool_wsum, 1)
                n, halves = n // 2, wo_sum
            query_rest(0, 0)
            query_rest(0, 1)
            split_expert(0)
            split_expert(1)
            rstds(1, 0)
            for h in range(2, H):
                query_rest(0, h)
                split_expert(h)
            query_rest(1, 0)
            query_rest(1, 1)
            split_expert(E - 1)
            rstds(2, 0)
            query_rest(1, 2)
            rstds(0, 1)
            for h in range(3, H):
                query_rest(1, h)
            query_rest(2, 0)
            with pool.Fori(2, B - 1) as b:
                body(b, False)
            body(B - 1, True)
            dispatch(B - 2, 0, SCATTERS)
            release(B - 2)
            rstds(B - 1, 1)

            def results(g, i):
                pool.wait_ge(m_ys, g * NX + i + 1)
                if not isinstance(g, int):
                    passed(pool)
                pool.indirect_dma_start(
                    y_dram[:, :], bass.IndirectOffsetOnAxis(ap=xs[:, i, D:D + 1].bitcast(I32), axis=0),
                    ys[:, i, :], None).then_inc(y_out[i], 16)

            for i in range(NX):
                if i == 6:
                    pool.wait_ge(dve_gap, B)
                    pool.tensor_tensor(e2[:, :], euler[:, :], gap[:, :], ALU.pow).then_inc(pool_e2, 1)
                results(0, i)
            for i in range(NX):
                if 3 <= i < 3 + SCATTERS // 2:
                    dispatch(B - 1, 2 * (i - 3), 2 * (i - 3) + 2)
                results(1, i)
            with pool.Fori(2, GROUPS) as g:
                for i in range(NX):
                    results(g, i)

        @block.tensor
        def _(pe):
            def pairs(out, w, x, rest=None):
                pe.matmul(out, w[0], x[0], start=True, stop=False)
                pe.matmul(out, w[1], x[0], start=False, stop=False)
                if rest is not None:
                    pe.wait_ge(*rest)
                return pe.matmul(out, w[0], x[1], start=False, stop=True)

            def cols(pair, a, b):
                return [t[:, a:b] for t in pair]

            def project_x(b, first):
                pe.wait_ge(dve_xn, b + 1)
                if not first:
                    pe.wait_ge(dve_lg, b - 1)
                for t in range(QT):
                    last = pe.transpose(b_bank[:, t * 128:(t + 1) * 128], xn[:, t, :], ident)
                last.then_inc(pe_xnT, 1)

            def project_k(b):
                pe.wait_ge(act_xnT, b + 1)
                if not isinstance(b, int) or b > 0:
                    pe.wait_ge(dve_q, 8 * b)
                pairs(a_bank[:, :], cols(wk_sb, 0, D), cols(xnT, 0, T), (dve_xl, b + 1)).then_inc(pe_k, 1)

            def values(b):
                for n, (kt, i) in enumerate(VW_ORDER):
                    if kt == 0 and isinstance(b, int) and b == 0:
                        pe.wait_ge(dve_wlo, 3 + i)
                    if kt > 1:
                        pe.wait_ge((act_vw, dve_vw)[i], 4 * b + kt - 1)
                    elif (kt, i) == (0, 1):
                        pe.wait_ge(dve_q, 8 * b + 3)
                    out_bank = (t_bank, (a_bank, b_bank))[i][kt % 2]
                    pairs(out_bank[:, :], cols(xnT, kt * 128, (kt + 1) * 128),
                          cols(wvo_sb, i * 512, (i + 1) * 512)).then_inc(pe_vw, 1)

            def queries(b, h):
                if h == 0:
                    pe.wait_ge(dve_kT, b + 1)
                elif h == 3:
                    pe.wait_ge(dve_vw, 4 * b + 3)
                else:
                    pe.wait_ge(dve_q, 8 * b + h)
                pairs(a_bank[:, :], cols(wq_sb, h * D, (h + 1) * D), cols(xnT, 0, T)).then_inc(pe_q, 1)

            def scores(b, h, qt, odd):
                w = (qt + 1) * 128
                if qt == 0:
                    pe.wait_ge(dve_q, 8 * b + h + 1)
                    ins = pe.matmul(s_bank[0], qT_in[:, h % 2, 0:128], kT_in[:, odd, 0:w], start=True, stop=True)
                else:
                    if qt == 1:
                        pe.wait_ge(pool_ql, 8 * b + h + 1)
                        if h == 0:
                            pe.wait_ge(dve_kl, b + 1)
                    ins = pairs(s_bank[qt], [q[:, h % 2, qt * 128:w] for q in qT],
                                [k[:, odd, 0:w] for k in kT])
                ins.then_inc(pe_s, 1)

            def transposes(b, h, qt):
                n = 32 * b + 4 * h + qt
                if h == 0 and qt < 2:
                    pe.wait_ge(act_vw, 4 * b + 3 + qt)
                else:
                    pe.wait_ge(act_pT, n - 1)
                pe.wait_ge(dve_pn, n + 1)
                for kt in range(qt + 1):
                    last = pe.transpose(t_bank[qt % 2][:, kt * 128:(kt + 1) * 128],
                                        pr[:, h % 2, PR[qt] + kt * 128:PR[qt] + (kt + 1) * 128], ident)
                last.then_inc(pe_t, 1)

            def attend(b, h, first):
                pe.wait_ge(act_pT, 32 * b + 4 * h + 3)
                if h == 0:
                    pe.wait_ge(dve_vw, 4 * b + 4)
                    if not first:
                        pe.wait_ge(act_oT, b)
                q3 = (QT - 1) * 128
                for kt in range(QT - 1):
                    pe.matmul(o_bank[:, kt * 128:q3], vw[:, kt, h * D:(h + 1) * D],
                              pT[:, h % 2, kt, kt * 128:q3], start=(h == 0 and kt == 0),
                              stop=False)
                pe.wait_ge(act_pT, 32 * b + 4 * h + 4)
                for kt in range(QT):
                    last = pe.matmul(o_bank[:, q3:], vw[:, kt, h * D:(h + 1) * D],
                                     pT[:, h % 2, kt, q3:], start=False,
                                     stop=(h == H - 1 and kt == QT - 1))
                last.then_inc(pe_av, 1)

            def residual(b, in_body):
                pe.wait_ge(act_oT, b + 1)
                if in_body:
                    pe.wait_ge(dve_vw, 4 * b + 8)
                for t in range(QT):
                    last = pe.transpose(r_bank(b)[:, t * 128:(t + 1) * 128], oT[:, t * 128:(t + 1) * 128], ident)
                last.then_inc(pe_x2, 1)

            def normed(b):
                pe.wait_ge(dve_x2n, b + 1)
                for t in range(QT):
                    last = pe.transpose(r_bank(b)[:, t * 128:(t + 1) * 128], payload[:, t, 0, 0:D], ident)
                last.then_inc(pe_xn2T, 1)

            def logits(b):
                pe.wait_ge(act_xn2T, b + 1)
                for t in range(QT):
                    last = pe.matmul(r_bank(b)[:, t * E:(t + 1) * E], xn2T[:, t * 128:(t + 1) * 128], wr_sb[:, :],
                                     start=True, stop=True)
                last.then_inc(pe_lg, 1)

            def ranks(b, in_body):
                if in_body:
                    pe.wait_ge(dve_xl, b + 3)
                pe.wait_ge(dve_oh, b + 1)
                w = QT * E
                rb = r_bank(b)
                pe.matmul(rb[:, 64:64 + w], lt_bf[:, :], oh_bf[:, :], start=True, stop=False)
                for t in range(1, QT):
                    pe.matmul(rb[:, 64 + t * E:64 + w], one_bf[:, :], oh_bf[:, 0:w - t * E],
                              start=False, stop=(t == QT - 1))
                for t in range(QT):
                    last = pe.matmul(rb[:, 128:128 + E], one_bf[:, :], oh_bf[:, t * E:(t + 1) * E],
                                     start=(t == 0), stop=(t == QT - 1))
                last.then_inc(pe_cnt, 1)

            def value_weights(i):
                pe.matmul(wvo_bank[i][:, :], wvT, wo_in[:, i * 512:(i + 1) * 512],
                          start=True, stop=True).then_inc(pe_wvo, 1)
                if i == 1:
                    pe.wait_ge(pool_wsum, 3)
                    pe.matmul(o_bank[:, 0:1], wo_sum[:, 0:D], bkv_sb[:, 1:2],
                              start=True, stop=True).then_inc(pe_bvo, 1)

            def body(b, first, last, odd):
                for s in range(H):
                    prev = (b, s - 1) if s else (b - 1, H - 1)
                    behind = s > 0 or not first
                    if 0 < s < H - 2:
                        queries(b, s + 2)
                    if behind:
                        transposes(*prev, 0)
                        transposes(*prev, 1)
                    scores(b, s, 0, odd)
                    scores(b, s, 1, odd)
                    if behind:
                        transposes(*prev, 2)
                    scores(b, s, 2, odd)
                    if behind:
                        transposes(*prev, 3)
                    scores(b, s, 3, odd)
                    if not first and s == 4:
                        logits(b - 1)
                    if not first and s == (H - 2 if last else H - 1):
                        ranks(b - 1, not last)
                    if not last:
                        if s == H - 3:
                            project_x(b + 1, first)
                        if s == H - 2:
                            project_k(b + 1)
                    if behind:
                        attend(*prev, first or s == 0)
                    if s == 0:
                        if first:
                            value_weights(1)
                        queries(b, 2)
                        values(b)
                    if not first and s == 1:
                        residual(b - 1, True)
                    if not first and s == 3:
                        normed(b - 1)
                    if s >= H - 2 and not last:
                        queries(b + 1, s - (H - 2))

            pe.wait_ge(ld_kv, LD_KV)
            project_x(0, True)
            pe.transpose(o_bank[:, 0:D], wkv_in[:, D:2 * D], ident).then_inc(pe_wvT, 1)
            pe.wait_ge(dve_wlo, 1)
            project_k(0)
            pe.wait_ge(dve_wlo, 2)
            queries(0, 0)
            pe.wait_ge(act_wvT, 1)
            pe.wait_ge(ld_o, LD_O)
            value_weights(0)
            queries(0, 1)
            body(0, True, False, 0)
            with pe.Fori(1, B - 2, 2) as b:
                body(b, False, False, 1)
                body(b + 1, False, False, 0)
            body(B - 1, False, True, 1)
            for qt in range(QT):
                transposes(B - 1, H - 1, qt)
            def flat(w):
                return w[:, :, :].rearrange("p e n -> p (e n)")
            wgu_flat = [flat(w) for w in wgu_sb]
            wd_flat = wd_sb[:, :, :, :].rearrange("p e c n -> p (e c n)")

            def experts(j, n):
                return nc.values_load_multi_w_load_instructions(
                    e_tab[0:1, bass.ds(j, n)], engines=(mybir.EngineType.PE,), min_val=0, max_val=E - 1,
                    skip_runtime_bounds_check_because="VectorE clamps them to the experts")[1]

            def m_transpose(g, i):
                pe.wait_ge(xs_in[i], g * 16 + 16)
                if not (isinstance(g, int) and g * NX + i == 0):
                    pe.wait_ge(m_xTl, g * NX + i)
                pe.transpose(bank[0][:, 0:D], xs[:, i, 0:D], ident).then_inc(m_xT, 1)

            def m_product(g, i, e, up):
                if not up:
                    pe.wait_ge(m_xTl, g * NX + i + 1)
                at = e * (2 * I) + (I if up else 0)
                pairs(bank[(4 if up else 2) + i % 2][:, 0:I], [x[:, i % 2, :] for x in xsT],
                      [w[:, bass.ds(at, I)] for w in wgu_flat]).then_inc(m_u if up else m_g, 1)

            def m_hidden_t(g, i):
                j = g * NX + i
                pe.wait_ge(m_hid, j + 1)
                if not (isinstance(g, int) and j < 1):
                    pe.wait_ge(m_hTc, j)
                for c in range(IC):
                    last = pe.transpose(bank[6][:, c * 128:(c + 1) * 128],
                                        hid[:, i % 2, c * 128:(c + 1) * 128], ident)
                last.then_inc(m_hT, 1)

            def m_down(g, i, e, last_tile=False):
                j = g * NX + i
                if last_tile:
                    pe.wait_ge(m_hTc, j + 1)
                if not (isinstance(g, int) and j < 1):
                    pe.wait_ge(m_ys, j)
                for c in range(IC):
                    last = pe.matmul(bank[7][:, 0:D], hidT[:, i % 2, c * 128:(c + 1) * 128],
                                     wd_flat[:, bass.ds(e * (IC * D) + c * D, D)], start=(c == 0),
                                     stop=(c == IC - 1))
                last.then_inc(m_y, 1)

            def tile(g, i):
                return (g + i // NX, i % NX)

            def expert_group(g, first, last):
                for i in range(NX):
                    if i % 4 == 0:
                        e = (list(e) if i else []) + list(experts(g * NX + i, 4))
                    if not (last and i == NX - 1):
                        m_transpose(*tile(g, i + 1))
                    m_product(g, i, e[i], False)
                    if i == 0 and not first:
                        old = experts(g * NX - 2, 2)
                    if first and i == 1:
                        pe.wait_ge(act_oT, B)
                    m_product(g, i, e[i], True)
                    if not (first and i == 0):
                        m_hidden_t(*tile(g, i - 1))
                    if not (first and i < 2):
                        m_down(*tile(g, i - 2), old[i] if i < 2 else e[i - 2])
                    if isinstance(g, int):
                        if (g, i) == (0, 0):
                            residual(B - 1, False)
                        elif (g, i) == (0, 4):
                            normed(B - 1)
                        elif (g, i) == (0, 5):
                            logits(B - 1)
                        elif (g, i) == (1, 1):
                            ranks(B - 1, False)

            pe.wait_ge(dve_tab, 1)
            pe.wait_ge(ld_moe, LD_MOE)
            pe.wait_ge(pool_gu, E)
            m_transpose(0, 0)
            attend(B - 1, H - 1, False)
            expert_group(0, True, False)
            expert_group(1, False, False)
            pe.wait_ge(dve_tab, 3)
            with pe.Fori(2, GROUPS - 1) as g:
                expert_group(g, False, False)
            expert_group(GROUPS - 1, False, True)
            old = experts(TILES - 2, 2)
            m_hidden_t(GROUPS - 1, NX - 1)
            m_down(GROUPS - 1, NX - 2, old[0])
            m_down(GROUPS - 1, NX - 1, old[1], last_tile=True)

        @block.scalar
        def _(act):
            def project_x(b):
                act.wait_ge(pe_xnT, b + 1)
                act.copy(xnT[0][:, :], b_bank[:, :]).then_inc(act_xnT, 1)

            def project_k(b, odd):
                act.wait_ge(dve_kT, b + 1)
                act.copy(kT[0][:, odd, :], kT_in[:, odd, :]).then_inc(act_kh, 1)

            def values(b, kt):
                act.wait_ge(pe_vw, 8 * b + VW_ORDER.index((kt, 0)) + 1)
                act.copy(vw[:, kt, 0:512], t_bank[kt % 2][:, :]).then_inc(act_vw, 1)

            def value_weights(i):
                act.wait_ge(pe_wvo, i + 1)
                act.copy(wvo_sb[0][:, i * 512:(i + 1) * 512], wvo_bank[i][:, :]).then_inc(act_whi, 1)
                if i == 1:
                    act.wait_ge(pe_bvo, 1)
                    act.copy(bvo[:, :], o_bank[:, 0:1])

            def output(b):
                act.wait_ge(pe_av, 8 * b + 8)
                act.activation(oT[:, :], o_bank[:, :], ACT.Identity, bias=bvo[:, 0:1]).then_inc(act_oT, 1)

            def queries(b, h):
                act.wait_ge(dve_q, 8 * b + h + 1)
                act.copy(qT[0][:, h % 2, :], qT_in[:, h % 2, :]).then_inc(act_qh, 1)

            def exps(b, h, qt):
                act.wait_ge(dve_negs, 32 * b + 4 * h + qt + 1)
                p = pr[:, h % 2, PR[qt]:PR[qt + 1]]
                act.activation(p, p, ACT.Exp,
                               bias=nmax[:, h % 2, qt:qt + 1], scale=-1.0,
                               accum_out=rsum[:, h % 2, qt:qt + 1]).then_inc(act_p, 1)

            def evacuate(b, h, qt, first):
                act.wait_ge(pe_t, 32 * b + 4 * h + qt + 1)
                if qt == 0 and not (first and h < 2):
                    act.wait_ge(pe_av, 8 * b + h - 1)
                act.copy(pT[:, h % 2, 0:qt + 1, qt * 128:(qt + 1) * 128],
                         t_bank[qt % 2][:, 0:(qt + 1) * 128].rearrange("p (k q) -> p k q", q=128)).then_inc(act_pT, 1)

            def normed(b):
                act.wait_ge(pe_xn2T, b + 1)
                act.copy(xn2T[:, :], r_bank(b)[:, :]).then_inc(act_xn2T, 1)

            def ratio(b):
                act.wait_ge(dve_gap, b + 1)
                act.activation(e2[:, :], gap[:, :], ACT.Exp).then_inc(act_e2, 1)

            def body(b, first, last, odd):
                for s in range(H):
                    prev = (b, s - 1) if s else (b - 1, H - 1)
                    behind = s > 0 or not first
                    if behind:
                        evacuate(*prev, 0, first)
                        evacuate(*prev, 1, first)
                    if 0 < s < H - 1:
                        queries(b, s + 1)
                    if s == 4 and not first:
                        normed(b - 1)
                    if behind:
                        evacuate(*prev, 2, first)
                    exps(b, s, 0)
                    exps(b, s, 1)
                    if behind:
                        evacuate(*prev, 3, first)
                    exps(b, s, 2)
                    exps(b, s, 3)
                    if s == 0 and first:
                        value_weights(1)
                    if s == 0:
                        queries(b, 1)
                    elif s == H - 1 and not last:
                        queries(b + 1, 0)
                    if s == 6 and not first:
                        ratio(b - 1)
                    if not last:
                        if s == H - 3:
                            project_x(b + 1)
                        if s == H - 2:
                            project_k(b + 1, 1 - odd)
                    if s == 0:
                        if not first:
                            output(b - 1)
                        for kt in range(QT):
                            values(b, kt)

            act.wait_ge(ld_kv, LD_KV)
            act.copy(wk_sb[0][:, :], wkv_in[:, 0:D]).then_inc(act_whi, 1)
            project_x(0)
            act.wait_ge(pe_wvT, 1)
            act.copy(wvT, o_bank[:, 0:D]).then_inc(act_wvT, 1)
            act.wait_ge(ld_q, LD_Q)
            act.copy(wq_sb[0][:, :], wq_in).then_inc(act_whi, 1)
            project_k(0, 0)
            queries(0, 0)
            value_weights(0)
            body(0, True, False, 0)
            with act.Fori(1, B - 2, 2) as b:
                body(b, False, False, 1)
                body(b + 1, False, False, 0)
            body(B - 1, False, True, 1)
            for qt in range(QT):
                evacuate(B - 1, H - 1, qt, False)
            act.preload_act_table(ACT.Silu)

            def m_rows(g, i):
                j = g * NX + i
                act.wait_ge(m_xT, j + 1)
                act.copy(xsT[0][:, i % 2, :], bank[0][:, 0:D]).then_inc(m_xTc, 1)

            def m_silu(g, i):
                j = g * NX + i
                act.wait_ge(m_g, j + 1)
                act.activation(sg[:, i % 2, :], bank[2 + i % 2][:, 0:I], ACT.Silu).then_inc(m_sg, 1)

            def m_result(g, i):
                j = g * NX + i
                act.wait_ge(m_y, j + 1)
                act.activation(ys[:, i, :], bank[7][:, 0:D], ACT.Copy,
                               scale=xs[:, i, D + 1:D + 2]).then_inc(m_ys, 1)

            def tile(g, i):
                return (g + i // NX, i % NX)

            def expert_group(g, first, last):
                for i in range(NX):
                    if not (last and i == NX - 1):
                        m_rows(*tile(g, i + 1))
                    m_silu(g, i)
                    if not (first and i < 2):
                        m_result(*tile(g, i - 2))
                    if isinstance(g, int):
                        if (g, i) == (0, 4):
                            normed(B - 1)

            m_rows(0, 0)
            output(B - 1)
            expert_group(0, True, False)
            expert_group(1, False, False)
            with act.Fori(2, GROUPS - 1) as g:
                expert_group(g, False, False)
            expert_group(GROUPS - 1, False, True)
            m_result(GROUPS - 1, NX - 2)
            m_result(GROUPS - 1, NX - 1)

        @block.vector
        def _(dve):
            count = {"base": 0, "n": 0}

            def link(ins):
                count["n"] += 1
                ins.then_inc(dve_step, 1)
                dve.wait_ge(dve_step, count["base"] + count["n"])

            def x_tile(b, t):
                return x_all[:, bass.ds(b * T + t * D, D)]

            def moments(b, which, st_, mv_):
                if not isinstance(b, int):
                    passed(dve)
                for t in range(QT):
                    ins = dve.bn_stats(st_[:, t, :], x_tile(b, t))
                link(ins)
                if not isinstance(b, int):
                    passed(dve)
                for t in range(QT):
                    ins = dve.bn_aggr(mv_[:, t, :], st_[:, t, :])
                link(ins)
                dve.tensor_scalar(veps[:, which, :], mv_[:, :, 1], EPS, None, ALU.add).then_inc(dve_var[which], 1)

            def norm_in(b):
                if not isinstance(b, int) or b > 0:
                    dve.wait_ge(pe_xnT, b)
                dve.wait_ge(pool_rstd[0], b + 1)
                for t in range(QT):
                    ins = dve.tensor_scalar(xn[:, t, :], x_tile(b, t), mv[:, t, 0:1], rstd[:, 0, t:t + 1],
                                            ALU.subtract, ALU.mult)
                ins.then_inc(dve_xn, 1)

            def x_rest(b):
                dve.wait_ge(act_xnT, b + 1)
                dve.tensor_tensor(xnT[1][:, :], b_bank[:, :], xnT[0][:, :].bitcast(F32),
                                  ALU.subtract).then_inc(dve_xl, 1)

            def keys(b, odd):
                dve.wait_ge(pe_k, b + 1)
                dve.scalar_tensor_tensor(out=kT_in[:, odd, :], in0=a_bank[:, :], scalar=bkv_sb[:, 0:1],
                                         in1=pe_sb[:, :], op0=ALU.add, op1=ALU.add).then_inc(dve_kT, 1)

            def key_rest(b, odd):
                dve.wait_ge(act_kh, b + 1)
                dve.tensor_tensor(kT[1][:, odd, :], kT_in[:, odd, :], kT[0][:, odd, :].bitcast(F32),
                                  ALU.subtract).then_inc(dve_kl, 1)

            def values(b, kt):
                dve.wait_ge(pe_vw, 8 * b + VW_ORDER.index((kt, 1)) + 1)
                dve.tensor_copy(vw[:, kt, 512:1024], (a_bank, b_bank)[kt % 2][:, :]).then_inc(dve_vw, 1)

            def queries(b, h):
                dve.wait_ge(pe_q, 8 * b + h + 1)
                dve.scalar_tensor_tensor(out=qT_in[:, h % 2, :], in0=a_bank[:, :], scalar=bq_sb[:, h:h + 1],
                                         in1=pe_sb[:, :], op0=ALU.add, op1=ALU.add).then_inc(dve_q, 1)

            def masked(b, h, qt):
                n = 32 * b + 4 * h + qt
                dve.wait_ge(pe_s, n + (2 if qt == 0 else 1))
                w = (qt + 1) * 128
                if not isinstance(b, int):
                    passed(dve)
                dve.tensor_tensor_reduce(out=pr[:, h % 2, PR[qt]:PR[qt + 1]], in0=s_bank[qt],
                                         in1=cst[:, C_MASK + T - w:C_MASK + T], scale=-SCALE, scalar=BIG,
                                         op0=ALU.add, op1=ALU.min,
                                         accum_out=nmax[:, h % 2, qt:qt + 1]).then_inc(dve_negs, 1)

            def normalise(b, h):
                def inverse(q0, q1):
                    dve.wait_ge(act_p, 32 * b + 4 * h + q1)
                    count["n"] += 1
                    dve.reciprocal(rinv[:, h % 2, q0:q1], rsum[:, h % 2, q0:q1]).then_inc(dve_step, 1)

                def scale(qt):
                    p = pr[:, h % 2, PR[qt]:PR[qt + 1]]
                    dve.tensor_scalar(p, p, rinv[:, h % 2, qt:qt + 1], None, ALU.mult).then_inc(dve_pn, 1)
                inverse(0, 3)
                dve.wait_ge(dve_step, count["base"] + count["n"])
                scale(0)
                scale(1)
                inverse(3, 4)
                scale(2)
                dve.wait_ge(dve_step, count["base"] + count["n"])
                scale(3)

            def residual(b):
                dve.wait_ge(pe_x2, b + 1)
                xb = x_all[:, bass.ds(b * T, T)]
                link(dve.tensor_tensor(xb, r_bank(b)[:, :], xb, ALU.add))

            def norm_mid(b):
                dve.wait_ge(rows_free, b + 1)
                dve.wait_ge(pool_rstd[1], b + 1)
                for t in range(QT):
                    dve.tensor_scalar(payload[:, t, :, 0:D],
                                      x_tile(b, t).rearrange("p (o d) -> p o d", o=1).broadcast_to((128, TOPK, D)),
                                      mv2[:, t, 0:1], rstd[:, 1, t:t + 1], ALU.subtract, ALU.mult)
                d = payload[:, :, :, D].bitcast(I32)
                dve.tensor_scalar(d, d, T, None, ALU.add).then_inc(dve_x2n, 1)

            def e3(ap):
                return ap.rearrange("p (t e) -> p t e", e=E)

            def b3(ap):
                return ap.rearrange("p (t o) -> p t o", o=1).broadcast_to((128, QT, E))

            def choose(b, k):
                if k == 0:
                    dve.wait_ge(pe_lg, b + 1)
                    dve.tensor_copy(lg[:, 0, :], r_bank(b)[:, 0:QT * E]).then_inc(dve_lg, 1)
                    dve.wait_ge(dve_lg, b + 1)
                link(dve.reduce_max(top[:, k, :], e3(lg[:, k, :]), AX.X))
                link(dve.tensor_tensor(e3(iseq[:, :]), e3(lg[:, k, :]), b3(top[:, k, :]), ALU.is_ge))
                link(dve.tensor_tensor(key[:, :], iseq[:, :], cst[:, C_REV:C_REV + QT * E], ALU.mult))
                link(dve.reduce_max(kmax[:, :], e3(key[:, :]), AX.X))
                link(dve.tensor_tensor(e3(oh[:, k, :]), e3(key[:, :]), b3(kmax[:, :]), ALU.is_equal))
                if k == 0:
                    link(dve.scalar_tensor_tensor(out=lg[:, 1, :], in0=oh[:, 0, :], scalar=-BIG,
                                                  in1=lg[:, 0, :], op0=ALU.mult, op1=ALU.add))
                else:
                    dve.tensor_tensor(oh_bf[:, :], oh[:, 0, :], oh[:, 1, :], ALU.add).then_inc(dve_oh, 1)
                    dve.tensor_tensor(gap[:, :], top[:, 1, :], top[:, 0, :], ALU.subtract).then_inc(dve_gap, 1)

            def place(b):
                if isinstance(b, int) and b == B - 1:
                    dve.wait_ge(pool_e2, 1)
                else:
                    dve.wait_ge(act_e2, b + 1)
                dve.tensor_scalar(den[:, :], e2[:, :], 1.0, None, ALU.add)
                dve.wait_ge(pe_cnt, b + 1)
                link(dve.tensor_tensor(
                    e3(pos[:, :]), e3(r_bank(b)[:, 64:64 + QT * E]),
                    fill[:, :].rearrange("p (o e) -> p o e", o=1).broadcast_to((128, QT, E)), ALU.add))
                dve.reciprocal(wrow[:, :, 0], den[:, :])
                link(dve.tensor_tensor(
                    posk[:, :, :], oh[:, :, :],
                    pos[:, :].rearrange("p (o n) -> p o n", o=1).broadcast_to((128, TOPK, QT * E)), ALU.mult))
                dve.tensor_tensor(wrow[:, :, 1], e2[:, :], wrow[:, :, 0], ALU.mult)
                link(dve.reduce_sum(slot_f[:, :, :].rearrange("p k t -> p (k t)"),
                                    posk[:, :, :].rearrange("p k (t e) -> p (k t) e", e=E), AX.X))
                dve.tensor_copy(payload[:, :, :, D + 1], wrow[:, :, :])
                link(dve.tensor_tensor(fill[:, :], fill[:, :], r_bank(b)[:, 128:128 + E], ALU.add))
                dve.tensor_copy(slot[:, :, :], slot_f[:, :, :]).then_inc(dve_slot, 1)

            def wide(ap, n):
                return ap.rearrange("p (m o) -> p m o", o=1).broadcast_to((128, ap.shape[1], n))

            def tall(ap, n):
                return ap.rearrange("p (o m) -> p o m", o=1).broadcast_to((128, n, ap.shape[1]))

            def expert_tiles(early):
                link(dve.tensor_tensor(cnt[:, :], fill[:, :], cst[:, C_CAP:C_CAP + E], ALU.subtract))
                if early:
                    link(dve.tensor_scalar(cnt[:, :], cnt[:, :], -127.0, None, ALU.add))
                link(dve.tensor_tensor(over[:, :].rearrange("p (e m) -> p e m", m=NT), wide(cnt[:, :], NT),
                                       tall(cst[:, C_THR:C_THR + NT], E), ALU.is_gt))
                link(dve.reduce_sum(ntile[:, :], over[:, :].rearrange("p (e m) -> p e m", m=NT), AX.X))
                if not early:
                    link(dve.tensor_tensor(ntile[:, :], ntile[:, :], taken[:, 0:E], ALU.subtract))
                link(dve.tensor_tensor(cumm[:, :].rearrange("p (e f) -> p e f", f=E),
                                       cst[:, C_LE:C_LE + E * E].rearrange("p (e f) -> p e f", f=E),
                                       tall(ntile[:, :], E), ALU.mult))
                link(dve.reduce_sum(cum[:, :], cumm[:, :].rearrange("p (e f) -> p e f", f=E), AX.X))

            def tile_experts(n):
                j3 = done[:, 0:n * E].rearrange("p (j e) -> p j e", e=E)
                link(dve.tensor_tensor(j3, tall(cum[:, :], n), wide(cst[:, C_J:C_J + n], E), ALU.is_le))
                link(dve.reduce_sum(ej[:, 0:n], j3, AX.X))

            def tile_skips(early, n):
                j3 = done[:, 0:n * E].rearrange("p (j e) -> p j e", e=E)
                k3 = skip[:, 0:n * E].rearrange("p (j e) -> p j e", e=E)
                link(dve.tensor_tensor(k3, j3, tall(ntile[:, :] if early else rise[:, :], n), ALU.mult))
                link(dve.reduce_sum(st[:, 0:n], k3, AX.X))

            def tile_rows(early, n):
                at = 0 if early else EARLY
                link(dve.tensor_tensor(st[:, 0:n], cst[:, C_J:C_J + n], st[:, 0:n], ALU.subtract))
                if early:
                    link(dve.tensor_scalar(st[:, 0:n], st[:, 0:n], 128.0, None, ALU.mult))
                else:
                    link(dve.tensor_scalar(st[:, 0:n], st[:, 0:n], taken[:, 0:1], 128.0, ALU.add, ALU.mult))
                link(dve.scalar_tensor_tensor(out=rowf[:, 0:n], in0=ej[:, 0:n], scalar=float(CAP), in1=st[:, 0:n],
                                              op0=ALU.mult, op1=ALU.add))
                dve.tensor_copy(row_tab[:, at:at + n], rowf[:, 0:n])
                dve.tensor_scalar(e_tab[:, at:at + n], ej[:, 0:n], float(E - 1), None, ALU.min).then_inc(dve_tab, 1)

            def early_tiles():
                link(dve.memset(upto[:, 0:1], 0.0))
                link(dve.tensor_scalar(upto[:, 1:E + 1], cum[:, :], float(EARLY), None, ALU.min))
                dve.memset(taken[:, E:E + 1], 0.0)
                link(dve.tensor_tensor(taken[:, 0:E], upto[:, 1:E + 1], upto[:, 0:E], ALU.subtract))

            def late_rise():
                link(dve.tensor_tensor(rise[:, :], taken[:, 0:E], taken[:, 1:E + 1], ALU.subtract))
                link(dve.tensor_tensor(rise[:, :], rise[:, :], ntile[:, :], ALU.add))

            def value_weights_rest(i):
                dve.wait_ge(act_whi, 3 + i)
                w = slice(i * 512, (i + 1) * 512)
                dve.tensor_tensor(wvo_sb[1][:, w], wvo_bank[i][:, :], wvo_sb[0][:, w].bitcast(F32),
                                  ALU.subtract).then_inc(dve_wlo, 1)

            def body(b, first, last, odd):
                at = count["n"]
                for s in range(H):
                    for qt in range(QT):
                        masked(b, s, qt)
                    if s == 0:
                        queries(b, 1)
                    elif s + 2 < H:
                        queries(b, s + 2)
                    elif s == H - 2 and not last:
                        keys(b + 1, 1 - odd)
                    elif s == H - 1 and not last:
                        queries(b + 1, 0)
                    normalise(b, s)
                    if s == 0:
                        queries(b, 2)
                    if s == 0 and first:
                        value_weights_rest(1)
                    if s == 0:
                        for kt in range(QT):
                            values(b, kt)
                    if not last:
                        if s == 0:
                            moments(b + 1, 0, stats, mv)
                        if s == 3:
                            norm_in(b + 1)
                        if s == H - 3:
                            x_rest(b + 1)
                        if s == H - 2:
                            key_rest(b + 1, 1 - odd)
                    if not first:
                        if s == 1:
                            residual(b - 1)
                            moments(b - 1, 1, stats2, mv2)
                        if s == 2:
                            norm_mid(b - 1)
                        if s == 4:
                            choose(b - 1, 0)
                        if s == 5:
                            choose(b - 1, 1)
                        if last and s == 0:
                            expert_tiles(True)
                        if last and s == 3:
                            tile_experts(EARLY)
                            tile_skips(True, EARLY)
                            tile_rows(True, EARLY)
                        if last and s == 5:
                            early_tiles()
                        if s == (H - 2 if last else H - 1):
                            place(b - 1)
                assert first or last or count["n"] - at == STEPS

            dve.wait_ge(ld_x0, 16)
            moments(0, 0, stats, mv)
            norm_in(0)

            def weight_rest(n, w, w_in):
                dve.wait_ge(act_whi, n + 1)
                dve.tensor_tensor(w[1][:, :], w_in, w[0][:, :].bitcast(F32), ALU.subtract).then_inc(dve_wlo, 1)
            weight_rest(0, wk_sb, wkv_in[:, 0:D])
            x_rest(0)
            weight_rest(1, wq_sb, wq_in)
            keys(0, 0)
            key_rest(0, 0)
            queries(0, 0)
            dve.wait_ge(ld_o, LD_O)
            dve.tensor_copy(lt_bf[:, :], cst[:, C_LT:C_LT + 128])
            dve.memset(one_bf[:, :], 1.0)
            dve.tensor_copy(fill[:, :], cst[:, C_CAP:C_CAP + E])
            link(dve.tensor_copy(payload[:, :, :, D].bitcast(I32),
                                 dst0[:, 0:SCATTERS].rearrange("p (t k) -> p t k", k=TOPK)))
            dve.wait_ge(pad_zero, 1)
            dve.tensor_copy(padrows[:, :, D].bitcast(I32), dst0[:, SCATTERS:]).then_inc(pad_ready, 1)
            value_weights_rest(0)
            dve.wait_ge(ld_x, 16 * (B - 1))
            body(0, True, False, 0)
            count["base"], count["n"] = count["n"], 0
            before = count["base"]
            with dve.Fori(1, B - 2, 2) as b:
                count["base"], count["n"] = (b - 1) * STEPS + before, 0
                body(b, False, False, 1)
                body(b + 1, False, False, 0)
            count["base"], count["n"] = before + (B - 2) * STEPS, 0
            body(B - 1, False, True, 1)
            def m_hidden(g, i):
                j = g * NX + i
                dve.wait_ge(m_sg, j + 1)
                dve.wait_ge(m_u, j + 1)
                dve.tensor_tensor(hid[:, i % 2, 0:I], sg[:, i % 2, :], bank[4 + i % 2][:, 0:I],
                                  ALU.mult).then_inc(m_hid, 1)

            def m_hidden_t(g, i):
                j = g * NX + i
                dve.wait_ge(m_hT, j + 1)
                dve.tensor_copy(hidT[:, i % 2, :], bank[6][:, 0:IP]).then_inc(m_hTc, 1)

            def m_rows_rest(g, i):
                dve.wait_ge(m_xTc, g * NX + i + 1)
                dve.tensor_tensor(xsT[1][:, i % 2, :], bank[0][:, 0:D], xsT[0][:, i % 2, :].bitcast(F32),
                                  ALU.subtract).then_inc(m_xTl, 1)

            def tile(g, i):
                return (g + i // NX, i % NX)

            def expert_group(g, first, last):
                for i in range(NX):
                    if not (last and i == NX - 1):
                        m_rows_rest(*tile(g, i + 1))
                    m_hidden(g, i)
                    if not (first and i == 0):
                        m_hidden_t(*tile(g, i - 1))
                    if isinstance(g, int):
                        if (g, i) == (0, 0):
                            residual(B - 1)
                        elif (g, i) == (0, 1):
                            moments(B - 1, 1, stats2, mv2)
                        elif (g, i) == (0, 3):
                            norm_mid(B - 1)
                        elif (g, i) == (0, 5):
                            choose(B - 1, 0)
                        elif (g, i) == (0, 7):
                            choose(B - 1, 1)
                        elif (g, i) == (1, 1):
                            place(B - 1)
                            dve.tensor_copy(fill_i[:, :], fill[:, :]).then_inc(dve_tab, 1)
                        elif (g, i) == (1, 2):
                            expert_tiles(False)
                        elif (g, i) == (1, 3):
                            late_rise()
                        elif (g, i) == (1, 4):
                            tile_experts(TILES - EARLY)
                        elif (g, i) == (1, 5):
                            tile_skips(False, TILES - EARLY)
                        elif (g, i) == (1, 6):
                            tile_rows(False, TILES - EARLY)

            m_rows_rest(0, 0)
            dve.wait_ge(pe_av, H * B)
            link(dve.memset(hid[:, :, I:IP], 0.0))
            expert_group(0, True, False)
            expert_group(1, False, False)
            with dve.Fori(2, GROUPS - 1) as g:
                expert_group(g, False, False)
            expert_group(GROUPS - 1, False, True)
            m_hidden_t(GROUPS - 1, NX - 1)

            for b in range(B):
                dve.wait_ge(y_ld[b], 16 * TOPK)
                xb = x_all[:, b * T:(b + 1) * T]
                link(dve.tensor_tensor(xb, xb, y_in[b][0], ALU.add))
                dve.tensor_tensor(xb, xb, y_in[b][1], ALU.add).then_inc(dve_fin, 1)


INPUTS = ("L0_attn_x", "L0_attn_Wq", "L0_attn_bq", "L0_attn_Wkv", "L0_attn_bkv", "L0_attn_Wo",
          "L0_ffn_Wr", "L0_ffn_Wg", "L0_ffn_Wu", "L0_ffn_Wd")


def kernel(**inputs):
    import concourse.bacc as bacc
    from concourse.bass_utils import run_bass_kernel_spmd

    nc = bacc.Bacc("TRN2", target_bir_lowering=False, num_devices=1)
    given = [(n, np.ascontiguousarray(inputs[n])) for n in INPUTS]
    given += list(zip(("consts", "dest", "positions"), constants()))
    given = [(n, np.ascontiguousarray(a.reshape(-1, D).T) if n in ("L0_attn_bq", "L0_attn_bkv") else a)
             for n, a in given]
    arrays, args = {}, []
    for name, a in given:
        arrays[name] = a
        args.append(nc.dram_tensor(name, a.shape, mybir.dt.from_np(a.dtype), kind="ExternalInput").ap())
    out = nc.dram_tensor("out", (B, T, D), F32, kind="ExternalOutput").ap()
    block_kernel(nc, *args, out)
    r = run_bass_kernel_spmd(nc, [arrays], core_ids=[0])
    return r.results[0]["out"]
```
